# Optimizing a Trainium2 kernel written in Bass

```python
import numpy as np
import jax
import jax.numpy as jnp

def _softmax(x, axis=-1):
    return jax.nn.softmax(x, axis=axis)

def _gelu(x):
    return jax.nn.gelu(x, approximate=True)

def _silu(x):
    return jax.nn.silu(x)

def _sigmoid(x):
    return jax.nn.sigmoid(x)

def _layernorm(x, axis=-1, eps=1e-05):
    m = jnp.mean(x, axis=axis, keepdims=True)
    v = jnp.var(x, axis=axis, keepdims=True)
    return (x - m) / jnp.sqrt(v + eps)

def _scatter_add(tgt, idx, src, axis=0):
    return tgt.at[idx].add(src)

def _segment_sum(src, seg, n):
    return jax.ops.segment_sum(src, seg, n)
kernel_name = 'mk_sandwich_d1_jaxref_r8_7fd5ac'

def setup_inputs(seed: int=0):
    np.random.seed(seed)
    _w = jnp.asarray

    def _L0_attn_setup():
        import jax, jax.numpy as jnp
        import numpy as np
        D_MODEL = 128
        D_STATE = 16
        D_CONV = 4
        D_INNER = 2 * D_MODEL
        BATCH = 2
        SEQ = 256
        LN_EPS = 1e-05

        def _layernorm(x, w, b):
            mu = jnp.mean(x, axis=-1, keepdims=True)
            var = jnp.mean(jnp.square(x - mu), axis=-1, keepdims=True)
            return (x - mu) * jax.lax.rsqrt(var + LN_EPS) * w + b

        def _forward(x, norm_w, norm_b, in_proj_w, conv_w, conv_b, x_proj_w, dt_w, dt_b, out_proj_w):
            residual = x
            xn = _layernorm(x, norm_w, norm_b)
            xz = xn @ in_proj_w.T
            x_in, z = jnp.split(xz, 2, axis=-1)
            x_conv = jax.lax.conv_general_dilated(jnp.swapaxes(x_in, 1, 2), conv_w, window_strides=(1,), padding=[(D_CONV - 1, 0)], dimension_numbers=('NCH', 'OIH', 'NCH'))
            x_conv = jnp.swapaxes(x_conv, 1, 2) + conv_b
            x_act = jax.nn.silu(x_conv)
            x_ssm = x_act @ x_proj_w.T
            delta_s = x_ssm[..., :1]
            B_mat = x_ssm[..., 1:1 + D_STATE].astype(jnp.float32)
            C = x_ssm[..., 1 + D_STATE:].astype(jnp.float32)
            delta = jax.nn.softplus(delta_s @ dt_w.T + dt_b).astype(jnp.float32)
            x_f32 = x_act.astype(jnp.float32)

            def step(h, inputs):
                d_t, b_t, c_t, u_t = inputs
                h = h * jnp.exp(-d_t)[..., None] + b_t[:, None, :] * u_t[..., None]
                y_t = jnp.einsum('bds,bs->bd', h, c_t)
                return (h, y_t)
            h0 = jnp.zeros((x.shape[0], D_INNER, D_STATE), jnp.float32)
            xs = (jnp.moveaxis(delta, 1, 0), jnp.moveaxis(B_mat, 1, 0), jnp.moveaxis(C, 1, 0), jnp.moveaxis(x_f32, 1, 0))
            _, y = jax.lax.scan(step, h0, xs)
            y = jnp.moveaxis(y, 0, 1).astype(x.dtype)
            return y * jax.nn.silu(z) @ out_proj_w.T + residual
        key = jax.random.key(seed)
        ks = jax.random.split(key, 10)
        s = lambda k, shape, fan: jax.random.normal(k, shape, jnp.float32) * (1.0 / np.sqrt(fan))
        return {'x': jax.random.normal(ks[0], (BATCH, SEQ, D_MODEL), jnp.float32), 'norm_w': jnp.ones((D_MODEL,), jnp.float32), 'norm_b': jnp.zeros((D_MODEL,), jnp.float32), 'in_proj_w': s(ks[1], (2 * D_INNER, D_MODEL), D_MODEL), 'conv_w': s(ks[2], (D_INNER, D_INNER, D_CONV), D_INNER * D_CONV), 'conv_b': s(ks[3], (D_INNER,), D_INNER * D_CONV), 'x_proj_w': s(ks[4], (2 * D_STATE + 1, D_INNER), D_INNER), 'dt_w': s(ks[5], (D_INNER, 1), 1), 'dt_b': s(ks[6], (D_INNER,), 1), 'out_proj_w': s(ks[7], (D_MODEL, D_INNER), D_INNER)}
    _L0_attn_in = _L0_attn_setup()

    def _L0_ffn_setup():
        import jax, jax.numpy as jnp
        import numpy as np
        B, N, D, F, E, K = (4, 256, 128, 512, 16, 2)
        EPS = 1e-05
        key = jax.random.key(seed)
        ks = jax.random.split(key, 6)
        scaled = lambda k, shape, fan: jax.random.normal(k, shape, jnp.float32) / np.float32(np.sqrt(fan))
        return {'x': jax.random.normal(ks[0], (B, N, D), jnp.float32), 'Wr': scaled(ks[1], (D, E), D), 'br': jnp.zeros((E,), jnp.float32), 'W1': scaled(ks[2], (E, D, F), D), 'W3': scaled(ks[3], (E, D, F), D), 'W2': scaled(ks[4], (E, F, D), F), 'gamma': jnp.ones((E, D), jnp.float32), 'beta': jnp.zeros((E, D), jnp.float32)}
    _L0_ffn_in = _L0_ffn_setup()
    _d = {'L0_attn_x': _L0_attn_in['x'], 'L0_attn_norm_w': _L0_attn_in['norm_w'], 'L0_attn_norm_b': _L0_attn_in['norm_b'], 'L0_attn_in_proj_w': _L0_attn_in['in_proj_w'], 'L0_attn_conv_w': _L0_attn_in['conv_w'], 'L0_attn_conv_b': _L0_attn_in['conv_b'], 'L0_attn_x_proj_w': _L0_attn_in['x_proj_w'], 'L0_attn_dt_w': _L0_attn_in['dt_w'], 'L0_attn_dt_b': _L0_attn_in['dt_b'], 'L0_attn_out_proj_w': _L0_attn_in['out_proj_w'], 'L0_ffn_Wr': _L0_ffn_in['Wr'], 'L0_ffn_br': _L0_ffn_in['br'], 'L0_ffn_W1': _L0_ffn_in['W1'], 'L0_ffn_W3': _L0_ffn_in['W3'], 'L0_ffn_W2': _L0_ffn_in['W2'], 'L0_ffn_gamma': _L0_ffn_in['gamma'], 'L0_ffn_beta': _L0_ffn_in['beta']}
    _x0 = _d['L0_attn_x']
    _d['L0_attn_x'] = jax.random.normal(jax.random.fold_in(jax.random.key(seed), 1), (16, 512, 128), dtype=_x0.dtype)
    del _x0
    return _d

def reference(L0_attn_x, L0_attn_norm_w, L0_attn_norm_b, L0_attn_in_proj_w, L0_attn_conv_w, L0_attn_conv_b, L0_attn_x_proj_w, L0_attn_dt_w, L0_attn_dt_b, L0_attn_out_proj_w, L0_ffn_Wr, L0_ffn_br, L0_ffn_W1, L0_ffn_W3, L0_ffn_W2, L0_ffn_gamma, L0_ffn_beta):

    def _L0_attn_ref(x, norm_w, norm_b, in_proj_w, conv_w, conv_b, x_proj_w, dt_w, dt_b, out_proj_w):
        import jax, jax.numpy as jnp
        import numpy as np
        D_MODEL = 128
        D_STATE = 16
        D_CONV = 4
        D_INNER = 2 * D_MODEL
        BATCH = 2
        SEQ = 256
        LN_EPS = 1e-05

        def _layernorm(x, w, b):
            mu = jnp.mean(x, axis=-1, keepdims=True)
            var = jnp.mean(jnp.square(x - mu), axis=-1, keepdims=True)
            return (x - mu) * jax.lax.rsqrt(var + LN_EPS) * w + b

        def _forward(x, norm_w, norm_b, in_proj_w, conv_w, conv_b, x_proj_w, dt_w, dt_b, out_proj_w):
            residual = x
            xn = _layernorm(x, norm_w, norm_b)
            xz = xn @ in_proj_w.T
            x_in, z = jnp.split(xz, 2, axis=-1)
            x_conv = jax.lax.conv_general_dilated(jnp.swapaxes(x_in, 1, 2), conv_w, window_strides=(1,), padding=[(D_CONV - 1, 0)], dimension_numbers=('NCH', 'OIH', 'NCH'))
            x_conv = jnp.swapaxes(x_conv, 1, 2) + conv_b
            x_act = jax.nn.silu(x_conv)
            x_ssm = x_act @ x_proj_w.T
            delta_s = x_ssm[..., :1]
            B_mat = x_ssm[..., 1:1 + D_STATE].astype(jnp.float32)
            C = x_ssm[..., 1 + D_STATE:].astype(jnp.float32)
            delta = jax.nn.softplus(delta_s @ dt_w.T + dt_b).astype(jnp.float32)
            x_f32 = x_act.astype(jnp.float32)

            def step(h, inputs):
                d_t, b_t, c_t, u_t = inputs
                h = h * jnp.exp(-d_t)[..., None] + b_t[:, None, :] * u_t[..., None]
                y_t = jnp.einsum('bds,bs->bd', h, c_t)
                return (h, y_t)
            h0 = jnp.zeros((x.shape[0], D_INNER, D_STATE), jnp.float32)
            xs = (jnp.moveaxis(delta, 1, 0), jnp.moveaxis(B_mat, 1, 0), jnp.moveaxis(C, 1, 0), jnp.moveaxis(x_f32, 1, 0))
            _, y = jax.lax.scan(step, h0, xs)
            y = jnp.moveaxis(y, 0, 1).astype(x.dtype)
            return y * jax.nn.silu(z) @ out_proj_w.T + residual
        return _forward(x, norm_w, norm_b, in_proj_w, conv_w, conv_b, x_proj_w, dt_w, dt_b, out_proj_w)

    def _L0_ffn_ref(x, Wr, br, W1, W3, W2, gamma, beta):
        import jax, jax.numpy as jnp
        import numpy as np
        B, N, D, F, E, K = (4, 256, 128, 512, 16, 2)
        EPS = 1e-05
        b, n, d = x.shape
        e = Wr.shape[1]
        xf = x.reshape(-1, d)
        logits = xf @ Wr + br
        probs = jax.nn.softmax(logits, axis=-1)
        vals, idx = jax.lax.top_k(probs, K)
        w = vals / vals.sum(axis=-1, keepdims=True)
        combine = jnp.zeros((xf.shape[0], e), x.dtype)
        for k in range(K):
            combine = combine + w[:, k:k + 1] * jax.nn.one_hot(idx[:, k], e, dtype=x.dtype)
        out = jnp.zeros_like(xf)
        for ei in range(e):
            h = jax.nn.silu(xf @ W1[ei]) * (xf @ W3[ei])
            y = h @ W2[ei]
            mu = y.mean(axis=-1, keepdims=True)
            var = ((y - mu) ** 2).mean(axis=-1, keepdims=True)
            y = (y - mu) * jax.lax.rsqrt(var + EPS) * gamma[ei] + beta[ei]
            out = out + combine[:, ei:ei + 1] * y
        return out.reshape(b, n, d)
    x = L0_attn_x
    x = x + _layernorm(_L0_attn_ref(_layernorm(x, axis=-1), L0_attn_norm_w, L0_attn_norm_b, L0_attn_in_proj_w, L0_attn_conv_w, L0_attn_conv_b, L0_attn_x_proj_w, L0_attn_dt_w, L0_attn_dt_b, L0_attn_out_proj_w), axis=-1)
    x = x + _layernorm(_L0_ffn_ref(_layernorm(x, axis=-1), L0_ffn_Wr, L0_ffn_br, L0_ffn_W1, L0_ffn_W3, L0_ffn_W2, L0_ffn_gamma, L0_ffn_beta), axis=-1)
    return x

_drawn_inputs = setup_inputs


def setup_inputs(seed=0):
    import zlib

    import numpy as np

    out = dict(_drawn_inputs(seed))
    spreads = {'L0_attn_norm_w': (1.0, 0.2),
     'L0_attn_norm_b': (0.0, 0.1),
     'L0_ffn_br': (0.0, 0.1),
     'L0_ffn_gamma': (1.0, 0.2),
     'L0_ffn_beta': (0.0, 0.1)}
    factors = {}
    for name, (base, spread) in spreads.items():
        noise = np.random.default_rng([zlib.crc32(name.encode()), seed]).standard_normal(out[name].shape)
        drawn = base * np.exp(spread * noise) if base else spread * noise
        out[name] = jnp.asarray(drawn.astype(out[name].dtype))
    for name, factor in factors.items():
        out[name] = (out[name] * factor).astype(out[name].dtype)
    return out
```

```python
import numpy as np
import concourse.bass as bass
from concourse import mybir
from contextlib import ExitStack

P = 128
SEQ = 512
D = 128
DI = 256
NST = 16
TAPS = 4
NT4 = SEQ // P
Q = 16
NBLK = SEQ // Q
CB = P // Q
HALVES = (1, 2, 4, 8)
NE = 16
EPS = 1e-5
DF = 512
FC = DF // P
ROW = D + 2
NOWHERE = 1 << 20

fp32 = mybir.dt.float32
f32r = mybir.dt.float32r
i32 = mybir.dt.int32
u32 = mybir.dt.uint32
bf16 = mybir.dt.bfloat16
ALU = mybir.AluOpType
ACT = mybir.ActivationFunctionType
AX = mybir.AxisListType


class Seq:

    def __init__(self, s, half, parity):
        self.s, self.half, self.parity = s, half, parity


class Chain:

    def __init__(self, eng, sem, per, seq):
        self.eng, self.sem, self.at, self.per, self.seq = eng, sem, 0, per, seq

    def link(self, ins):
        self.at += 1
        ins.then_inc(self.sem, 1)

    def wait(self):
        self.eng.wait_ge(self.sem, self.seq.s * self.per + self.at)

    def step(self, ins):
        self.link(ins)
        self.wait()

    def end(self):
        assert self.at == self.per, (self.at, self.per)


def wait_for(eng, sem, per, seq, k, ago=0):
    n = seq.s - ago
    if isinstance(n, int) and n < 0:
        return
    eng.wait_ge(sem, n * per + k)


def wait_past(eng, sem, value):
    if not (isinstance(value, int) and value <= 0):
        eng.wait_ge(sem, value)


def run_units(eng, ns, unit):
    seq = lambda n: Seq(n, n // 2, n % 2) if 0 <= n < ns else None
    for k in range(4):
        unit(seq(k), seq(k - 1), seq(k - 2))
    with eng.Fori(1, (ns - 2) // 2) as j:
        for p in range(2):
            unit(Seq(j * 2 + (2 + p), j + 1, p), Seq(j * 2 + (1 + p), j + p, 1 - p), Seq(j * 2 + p, j, p))
    for k in range(ns, ns + 2):
        unit(None, seq(k - 1), seq(k - 2))


def sandwich(nc, NS, x, norm_w, norm_b, in_wT, conv_wT, conv_b, x_wT, dt_w, dt_b, out_wT, masks, blockmask, ident_d,
             br, wr, w13, w2, gamma, beta, lower, iota_e, iota_t, token_id, out):
    NTOK = NS * NT4
    NTOKENS = NTOK * P
    NSLOT = (2 * NTOKENS + NE * (P - 1)) // P
    NSLOT += -NSLOT % 4
    NG = NTOK // NT4
    x1_d = nc.dram_tensor("x1_scratch", [NTOKENS, D], fp32).ap()
    xf_d = nc.dram_tensor("xf_scratch", [NTOKENS, D], fp32).ap()
    slots_d = nc.dram_tensor("slots_scratch", [NSLOT * P, ROW], fp32).ap()
    acc_d = nc.dram_tensor("acc_scratch", [NTOKENS, D], fp32).ap()
    ctx = ExitStack()
    early = ExitStack()
    with ctx:
        def sb(name, shape, dt=fp32):
            return (early if in_early[0] else ctx).enter_context(nc.sbuf_tensor(name, shape, dt))

        in_early = [False]

        def pb(name, shape, dt=fp32):
            return ctx.enter_context(nc.psum_tensor(name, shape, dt))

        def sem(name):
            return ctx.enter_context(nc.semaphore(name))

        ident = sb("ident", [P, P])
        neg_half = sb("neg_half", [P, NT4])
        top = sb("top", [P, NTOK, 2])
        topi = sb("topi", [P, NTOK, 2])
        blank = sb("blank", [P, 4, ROW])
        lower_b = sb("lower_b", [P, P], bf16)
        ones_b = sb("ones_b", [P, P], bf16)
        iota_es = sb("iota_es", [P, NE])
        iota_ts = sb("iota_ts", [1, NSLOT])
        tokid = sb("tokid", [P, NTOK])
        lower_f = sb("lower_f", [P, P])
        in_early[0] = True
        level_mask = sb("level_mask", [P, 5, P])
        block_mask = sb("block_mask", [P, CB])
        raw_w = sb("raw_w", [P, 2 * TAPS * DI])
        in_hi = sb("in_hi", [P, 4 * P], f32r)
        in_lo = sb("in_lo", [P, 4 * P], f32r)
        conv_hi = sb("conv_hi", [P, 2, TAPS, DI], f32r)
        conv_lo = sb("conv_lo", [P, 2, TAPS, DI], f32r)
        xproj = sb("xproj", [P, 2, 2 * NST + 1])
        outproj = sb("outproj", [P, 2, D])
        nw = sb("nw", [P, 1])
        nb = sb("nb", [P, 1])
        cbias = sb("cbias", [P, 2])
        dtw = sb("dtw", [P, 2])
        dtb = sb("dtb", [P, 2])
        ndtw = sb("ndtw", [P, 2])
        ndtb = sb("ndtb", [P, 2])
        brb = sb("brb", [P, NE])
        wr_sb = sb("wr_sb", [P, NE])

        xin = sb("xin", [P, 2, NT4, D])
        stats = sb("stats", [P, NT4, 6])
        mv1 = sb("mv1", [P, NT4, 2])
        ve1 = sb("ve1", [P, NT4])
        rs1 = sb("rs1", [P, NT4])
        mv2 = sb("mv2", [P, NT4, 2])
        ve2 = sb("ve2", [P, NT4])
        rs2 = sb("rs2", [P, NT4])
        xa = sb("xa", [P, 2, NT4, D])
        xb = sb("xb", [P, NT4, D])
        xn = sb("xn", [P, SEQ])
        xn_hi = sb("xn_hi", [P, SEQ], f32r)
        xn_lo = sb("xn_lo", [P, SEQ], f32r)
        xi_hi = sb("xi_hi", [P, 2, SEQ + 4], f32r)
        xi_lo = sb("xi_lo", [P, 2, SEQ + 4], f32r)
        u = sb("u", [P, 2, 2, SEQ])
        zs = sb("zs", [P, 2, 2, SEQ])
        xs = sb("xs", [P, 2, NT4, 2 * NST + 1])

        dec1 = sb("dec1", [P, 2, SEQ])
        dec2 = sb("dec2", [P, 2, SEQ // 2])
        dec4 = sb("dec4", [P, 2, SEQ // 4])
        dec8 = sb("dec8", [P, 2, SEQ // 8])
        dec16 = sb("dec16", [P, 2, SEQ // 16])
        pre = sb("pre", [P, 2, SEQ])
        R = sb("R", [P, 2, SEQ])
        RT = sb("RT", [P, 2, 2 * SEQ])
        BC = sb("BC", [P, 2, NT4, P])
        BCT = sb("BCT", [P, 2, SEQ])
        G = sb("G", [P, 5, SEQ])
        y = sb("y", [P, 2, SEQ])
        tmp = sb("tmp", [P, 2, SEQ])
        Sall = sb("Sall", [P, 2, NST, NBLK])
        decS = sb("decS", [P, 2, NST, NBLK])
        Hs = sb("Hs", [P, 1 + 2 * NST * NBLK])
        Hp = sb("Hp", [P, 2, NT4, P])
        HT = sb("HT", [P, 2 * SEQ])
        xr = sb("xr", [P, NT4, D])
        at = sb("at", [P, NT4, D])
        mv3 = sb("mv3", [P, NT4, 2])
        ve3 = sb("ve3", [P, NT4])
        rs3 = sb("rs3", [P, NT4])
        mv4 = sb("mv4", [P, NT4, 2])
        ve4 = sb("ve4", [P, NT4])
        rs4 = sb("rs4", [P, NT4])
        x1n = sb("x1n", [P, NT4, D])
        x1 = sb("x1", [P, NT4, D])
        xf = sb("xf", [P, NT4, D])
        xfT = sb("xfT", [P, SEQ])
        lg = sb("lg", [P, NT4, NE])
        top8 = sb("top8", [P, NT4, 8])
        topi8 = sb("topi8", [P, NT4, 8], u32)
        early.close()
        in_early[0] = False
        w2_sb = sb("w2_sb", [P, FC, NE, D])
        gb = sb("gb", [P, 2, NE, D])
        w13_sb = sb("w13_sb", [P, NE, 2, DF])
        m1 = sb("m1", [P, NTOK, NE])
        m2 = sb("m2", [P, NTOK, NE])
        m12 = sb("m12", [P, NTOK * NE], bf16)
        totals = sb("totals", [P, NE, NTOK])
        reset = sb("reset", [P, NE, NTOK])
        seen = sb("seen", [P, NE, NTOK])
        place = sb("place", [P, NTOK, NE])
        count_i = sb("count_i", [P, NE], i32)
        ntiles_i = sb("ntiles_i", [P, NE], i32)
        ntiles = sb("ntiles", [P, NE])
        tiles_to = sb("tiles_to", [P, NE])
        base = sb("base", [P, NE])
        ones_e = sb("ones_e", [P, NE])
        gap = sb("gap", [P, NTOK])
        pos = sb("pos", [P, NTOK, 2])
        meta = sb("meta", [P, NTOK, 2, 2])
        expert_f = sb("expert_f", [1, NSLOT])
        expert = sb("expert", [1, NSLOT], i32)
        send = sb("send", [P, 2, 2, ROW])
        send_at = sb("send_at", [P, 2, 2], i32)
        got = sb("got", [P, 4, ROW])
        got_id = sb("got_id", [P, 2], i32)
        xsT = sb("xsT", [P, 2, P])
        sil = sb("sil", [P, 2, DF])
        hid = sb("hid", [P, 2, DF])
        hidT = sb("hidT", [P, 2, DF])
        est = sb("est", [P, 6])
        emv = sb("emv", [P, 2, 2])
        eve = sb("eve", [P, 2])
        ers = sb("ers", [P, 2])
        erw = sb("erw", [P, 2])
        yn = sb("yn", [P, 2, D])
        yg = sb("yg", [P, 2, D])
        yo = sb("yo", [P, 2, D])
        facc = sb("facc", [P, 2, NT4, D])
        fx1 = sb("fx1", [P, 2, NT4, D])
        fst = sb("fst", [P, NT4, 6])
        fmv = sb("fmv", [P, NT4, 2])
        fve = sb("fve", [P, NT4])
        frs = sb("frs", [P, NT4])
        fn = sb("fn", [P, 2, NT4, D])
        fo = sb("fo", [P, 2, NT4, D])

        pA = pb("pA", [P, 2, SEQ])
        pB = pb("pB", [P, 2, SEQ])
        pR = pb("pR", [P, 2, SEQ])
        pY = pb("pY", [P, 2, SEQ])

        w_loaded = sem("w_loaded")
        in_w_loaded = sem("in_w_loaded")
        conv_w_loaded = sem("conv_w_loaded")
        const_ready = sem("const_ready")
        dve_consts = sem("dve_consts")
        w_hi = sem("w_hi")
        w_split = sem("w_split")
        x_loaded = [sem("x_loaded0"), sem("x_loaded1")]
        xr_loaded = sem("xr_loaded")
        x1_stored = sem("x1_stored")
        xf_stored = sem("xf_stored")
        lg_stored = sem("lg_stored")
        ds_t = sem("ds_t")
        bc_t = sem("bc_t")
        rt_t = sem("rt_t")
        g_mm = sem("g_mm")
        y_mm = sem("y_mm")
        xt_t = sem("xt_t")
        ip_mm = sem("ip_mm")
        cv_mm = sem("cv_mm")
        xs_mm = sem("xs_mm")
        op_mm = sem("op_mm")
        xf_t = sem("xf_t")
        lg_mm = sem("lg_mm")
        dec1_ready = sem("dec1_ready")
        bct_ready = sem("bct_ready")
        rt_ready = sem("rt_ready")
        y0_ready = sem("y0_ready")
        xn_ready = sem("xn_ready")
        xi_hi_ready = sem("xi_hi_ready")
        z_ready = sem("z_ready")
        u_ready = sem("u_ready")
        xs_ready = sem("xs_ready")
        s_ready = sem("s_ready")
        decs_ready = sem("decs_ready")
        hp_ready = sem("hp_ready")
        xft_ready = sem("xft_ready")
        r_odd_ready = sem("r_odd_ready")
        pre_ready = sem("pre_ready")
        rstd_a = sem("rstd_a")
        rstd_c = sem("rstd_c")
        xn_lo_ready = sem("xn_lo_ready")
        r_ready = sem("r_ready")
        dec_ready = sem("dec_ready")
        x1_ready = sem("x1_ready")
        dve_a = sem("dve_a")
        dve_b = sem("dve_b")
        dve_c = sem("dve_c")
        var_a = sem("var_a")
        var_c = sem("var_c")
        xa_ready = sem("xa_ready")
        xb_ready = sem("xb_ready")
        xi_lo_ready = sem("xi_lo_ready")
        bc_ready = sem("bc_ready")
        g_ready = sem("g_ready")
        y_read = sem("y_read")
        hs_ready = sem("hs_ready")
        yz_ready = sem("yz_ready")
        at_ready = sem("at_ready")
        x1n_ready = sem("x1n_ready")
        xf_ready = sem("xf_ready")
        lg_read = sem("lg_read")

        halves = lambda t, h: t.rearrange("p m (b k) -> p (m b) k", k=2 * h)
        x_v = x.rearrange("s (t p) d -> s p t d", p=P)
        x1_v = x1_d.rearrange("(s t p) d -> s p t d", p=P, t=NT4)
        xf_v = xf_d.rearrange("(s t p) d -> s p t d", p=P, t=NT4)

        q_blank, q_filled, q_acc_filled = sem("blank_ready"), sem("slots_filled"), sem("acc_filled")
        e_loaded = sem("e_loaded")
        pool_passed, dve_passed = sem("pool_passed"), sem("dve_passed")
        w13_loaded = sem("w13_loaded")
        w2_loaded = sem("w2_loaded")
        lower_ready = sem("lower_ready")
        lg_sum = sem("lg_sum")
        stage1_pe, stage1_act, stage1_pool = sem("stage1_pe"), sem("stage1_act"), sem("stage1_pool")
        stage1_dve = sem("stage1_dve")
        stage1_sp = sem("stage1_sp")
        route = sem("route")
        route_consts = sem("route_consts")
        gap_ready = sem("gap_ready")
        weights_ready = sem("weights_ready")
        m12_ready = sem("m12_ready")
        rank_mm = sem("rank_mm")
        pos_ready = sem("pos_ready")
        expert_ready = sem("expert_ready")
        send_loaded = [sem("send_loaded0"), sem("send_loaded1")]
        send_ready = sem("send_ready")
        sent = [sem("sent0"), sem("sent1")]
        got_loaded = [sem(f"got_loaded{q}") for q in range(4)]
        xs_t = sem("xs_t")
        xst_ready = sem("xst_ready")
        h1_mm, h3_mm, h_t, yo_mm = sem("h1_mm"), sem("h3_mm"), sem("h_t"), sem("yo_mm")
        sil_ready, hid_ready, hidt_ready = sem("sil_ready"), sem("hid_ready"), sem("hidt_ready")
        est_c = sem("est_c")
        evar_ready, erw_ready, epow = sem("evar_ready"), sem("erw_ready"), sem("epow")
        yn_ready, yg_ready, yo_ready = sem("yn_ready"), sem("yg_ready"), sem("yo_ready")
        id_ready = sem("id_ready")
        added = [sem("added0"), sem("added1")]
        f_loaded = [sem("f_loaded0"), sem("f_loaded1")]
        f_chain, f_var, f_rstd, f_n, f_o = sem("f_chain"), sem("f_var"), sem("f_rstd"), sem("f_n"), sem("f_o")
        f_stored = [sem("f_stored0"), sem("f_stored1")]

        block = ctx.enter_context(nc.Block())

        @block.sync
        def _(eng):
            for dst, src in ((ident[:, :], ident_d), (level_mask[:, :, :], masks), (block_mask[:, :], blockmask),
                             (xproj[:, :, :], x_wT.rearrange("(m p) f -> p m f", p=P)),
                             (outproj[:, :, :], out_wT.rearrange("(m p) f -> p m f", p=P)),
                             (nw[:, :], norm_w.rearrange("(p o) -> p o", o=1)), (nb[:, :], norm_b.rearrange("(p o) -> p o", o=1)),
                             (cbias[:, 0:1], conv_b[0:P].rearrange("(p o) -> p o", o=1)), (cbias[:, 1:2], conv_b[P:DI].rearrange("(p o) -> p o", o=1)),
                             (dtw[:, 0:1], dt_w[0:P, :]), (dtw[:, 1:2], dt_w[P:DI, :]),
                             (dtb[:, 0:1], dt_b[0:P].rearrange("(p o) -> p o", o=1)), (dtb[:, 1:2], dt_b[P:DI].rearrange("(p o) -> p o", o=1)),
                             (brb[:, :], br.rearrange("(o e) -> o e", o=1).broadcast_to([P, NE])), (wr_sb[:, :], wr)):
                eng.dma_start(dst, src).then_inc(w_loaded, 16)
            eng.dma_start(raw_w[:, 0:4 * P], in_wT).then_inc(in_w_loaded, 16)

            def load_x(a):
                wait_for(eng, xa_ready, 1, a, 1, ago=2)
                eng.dma_start(xin[:, a.parity, :, :], x_v[bass.ds(a.s, 1), :, :, :].rearrange("o p t d -> (o p) t d")).then_inc(x_loaded[a.parity], 16)

            for dst, src in ((iota_es[:, :], iota_e), (iota_ts[:, :], iota_t), (tokid[:, :], token_id), (lower_f[:, :], lower)):
                eng.dma_start(dst, src).then_inc(e_loaded, 16)
            load_x(Seq(0, 0, 0))
            eng.wait_ge(w_split, 1)
            eng.dma_start(raw_w[:, :], conv_wT).then_inc(conv_w_loaded, 16)
            load_x(Seq(1, 0, 1))
            eng.wait_ge(q_blank, 2)
            sv = slots_d.rearrange("(t p) f -> p t f", p=P)
            for t in range(0, NSLOT, 4):
                n = min(4, NSLOT - t)
                eng.dma_start(sv[:, t:t + n, :], blank[:, 0:n, :]).then_inc(q_filled, 16)
            for t in range(0, NTOK, 4):
                eng.dma_start(acc_d.rearrange("(t p) f -> p t f", p=P)[:, t:t + 4, :], blank[:, :, 0:D]).then_inc(q_acc_filled, 16)

            def unit(a, b, c):
                if a is not None and not (isinstance(a.s, int) and a.s < 2):
                    load_x(a)
                if c is not None:
                    wait_for(eng, x1_ready, 1, c, 1)
                    eng.dma_start(x1_v[bass.ds(c.s, 1), :, :, :].rearrange("o p t d -> (o p) t d"), x1[:, :, :]).then_inc(x1_stored, 16)
                    wait_for(eng, xf_ready, 1, c, 1)
                    eng.dma_start(xf_v[bass.ds(c.s, 1), :, :, :].rearrange("o p t d -> (o p) t d"), xf[:, :, :]).then_inc(xf_stored, 16)
                if b is not None:
                    wait_for(eng, x1_ready, 1, b, 1, ago=1)
                    eng.dma_start(xr[:, :, :], x_v[bass.ds(b.s, 1), :, :, :].rearrange("o p t d -> (o p) t d")).then_inc(xr_loaded, 16)

            run_units(eng, NS, unit)
            eng.wait_ge(x1_stored, 16 * NS)
            eng.wait_ge(xf_stored, 16 * NS)
            eng.nop().then_inc(stage1_sp, 1)
            eng.wait_ge(stage1_pe, 1)
            eng.wait_ge(stage1_act, 1)
            eng.wait_ge(stage1_pool, 1)
            eng.wait_ge(stage1_dve, 1)
            for k, v in enumerate((gamma, beta)):
                eng.dma_start(gb[:, k, :, :], v.rearrange("(o e) d -> o e d", o=1).broadcast_to([P, NE, D])).then_inc(w2_loaded, 16)
            eng.dma_start(w2_sb[:, :, :, :], w2).then_inc(w2_loaded, 16)
            eng.dma_start(w13_sb[:, :, :, :], w13).then_inc(w13_loaded, 16)
            def load_send(i, p):
                wait_past(eng, sent[p], i * 32)
                for k in range(2):
                    eng.dma_start(send[:, p, k, 0:D], xf_d.rearrange("(t p) d -> p t d", p=P)[:, bass.ds(i * 2 + p, 1), :].rearrange("p o d -> p (o d)")).then_inc(send_loaded[p], 16)

            for p in range(2):
                load_send(0, p)
            with eng.Fori(1, NTOK // 2) as i:
                for p in range(2):
                    load_send(i, p)
            for p in range(2):
                eng.wait_ge(sent[p], NTOK // 2 * 32)
            slots_v = slots_d.rearrange("(t p) f -> p t f", p=P)
            for q in range(4):
                eng.dma_start(got[:, q, :], slots_v[:, q, :]).then_inc(got_loaded[q], 16)
            with eng.Fori(1, NSLOT // 4) as j:
                for q in range(4):
                    eng.wait_ge(yo_ready, j * 4 + (q - 3))
                    eng.dma_start(got[:, q, :], slots_v[:, bass.ds(j * 4 + q, 1), :].rearrange("p o f -> p (o f)")).then_inc(got_loaded[q], 16)
            for p in range(2):
                eng.wait_ge(added[p], NSLOT // 2 * 16)
            av = acc_d.rearrange("(g t p) d -> g p t d", p=P, t=NT4)
            xv = x1_d.rearrange("(g t p) d -> g p t d", p=P, t=NT4)
            ov = out.rearrange("s (t p) d -> s p t d", p=P)

            def load_last(g, p):
                eng.dma_start(facc[:, p, :, :], av[bass.ds(g, 1), :, :, :].rearrange("o p t d -> (o p) t d")).then_inc(f_loaded[p], 16)
                eng.dma_start(fx1[:, p, :, :], xv[bass.ds(g, 1), :, :, :].rearrange("o p t d -> (o p) t d")).then_inc(f_loaded[p], 16)

            for p in range(2):
                load_last(p, p)
            for g in range(NG):
                eng.wait_ge(f_o, g + 1)
                eng.dma_start(ov[g, :, :, :], fo[:, g % 2, :, :]).then_inc(f_stored[g % 2], 16)
                if g + 2 < NG:
                    load_last(g + 2, g % 2)
            for p in range(2):
                eng.wait_ge(f_stored[p], 16 * (NG // 2))

        @block.gpsimd
        def _(eng):
            for t, v in ((neg_half[:, :], -0.5), (xi_hi[:, :, 0:TAPS - 1].bitcast(fp32), 0.0), (xi_lo[:, :, 0:TAPS - 1].bitcast(fp32), 0.0), (decS[:, :, :, 0:1], 0.0),
                         (Hs[:, 0:1], 0.0)):
                eng.memset(t, v).then_inc(const_ready, 1)
            eng.wait_ge(const_ready, 1)
            eng.memset(blank[:, :, :], 0.0).then_inc(q_blank, 1)
            eng.wait_ge(q_blank, 1)
            eng.memset(blank[:, :, D:D + 1], float(NOWHERE)).then_inc(q_blank, 1)

            def rstd(seq, k, ve, rs, var, done):
                wait_for(eng, var, 2, seq, k)
                eng.tensor_tensor(rs[:, :], ve[:, :], neg_half[:, :], ALU.pow).then_inc(done, 1)

            decs = [dec1, dec2, dec4, dec8, dec16]

            def decay(b, n):
                h = HALVES[n]
                src = halves(R[:, :, :] if n else u[:, b.parity, :, :], h)
                d = decs[n][:, :, :].rearrange("p m (b k) -> p (m b) k", k=2)
                if n == 0:
                    wait_for(eng, dec1_ready, 1, b, 1)
                    wait_for(eng, rt_t, 6, b, 5, ago=1)
                else:
                    wait_for(eng, r_ready, 4, b, n)
                    wait_for(eng, r_odd_ready, 1, b, 1)
                    wait_for(eng, dec_ready, 4, b, n)
                    wait_for(eng, rt_t, 6, b, n + 1)
                eng.tensor_tensor(halves(R[:, :, :], h)[:, :, 0:h], src[:, :, 0:h],
                                  d[:, :, 1:2].broadcast_to([P, SEQ // h, h]), ALU.mult).then_inc(r_ready, 1)
                if n == 3:
                    wait_for(eng, decs_ready, 1, b, 1, ago=1)
                eng.tensor_tensor(decs[n + 1][:, :, :].rearrange("p m (b o) -> p (m b) o", o=1), d[:, :, 0:1], d[:, :, 1:2],
                                  ALU.mult).then_inc(dec_ready, 1)

            def unit(a, b, c):
                if a is not None:
                    rstd(a, 1, ve1, rs1, var_a, rstd_a)
                if c is not None:
                    rstd(c, 1, ve3, rs3, var_c, rstd_c)
                if b is not None:
                    decay(b, 0)
                if a is not None:
                    rstd(a, 2, ve2, rs2, var_a, rstd_a)
                if a is not None:
                    wait_for(eng, xn_ready, 2, a, 2)
                    wait_for(eng, ip_mm, 4, a, 4, ago=1)
                    eng.tensor_tensor(xn_lo[:, :], xn[:, :], xn_hi[:, :].bitcast(fp32), ALU.subtract).then_inc(xn_lo_ready, 1)
                if b is not None:
                    decay(b, 1)
                if c is not None:
                    wait_for(eng, x1n_ready, 1, c, 1)
                    wait_for(eng, x1_stored, 16, c, 16, ago=1)
                    wait_for(eng, xr_loaded, 16, c, 16)
                    eng.tensor_tensor(x1[:, :, :], x1n[:, :, :], xr[:, :, :], ALU.add).then_inc(x1_ready, 1)
                if b is not None:
                    decay(b, 2)
                if c is not None:
                    rstd(c, 2, ve4, rs4, var_c, rstd_c)
                if b is not None:
                    decay(b, 3)

            run_units(eng, NS, unit)
            eng.wait_ge(rstd_c, 2 * NS)
            eng.wait_ge(dec_ready, 4 * NS)
            eng.wait_ge(xn_lo_ready, NS)
            eng.nop().then_inc(stage1_pool, 1)

            eng.wait_ge(pos_ready, 2)
            eng.wait_ge(weights_ready, 3)
            nfill = (NSLOT + 3) // 4
            eng.wait_ge(q_filled, 16 * nfill)
            eng.wait_ge(q_acc_filled, 16 * (NTOK // 4))

            def dispatch(i, p):
                wait_past(eng, sent[p], i * 32)
                eng.tensor_copy(send[:, p, :, D:D + 2], meta[:, bass.ds(i * 2 + p, 1), :, :].rearrange("p o k f -> p (o k) f")).then_inc(send_ready, 1)
                eng.tensor_copy(send_at[:, p, :], pos[:, bass.ds(i * 2 + p, 1), :].rearrange("p o k -> p (o k)")).then_inc(send_ready, 1)
                eng.wait_ge(send_ready, i * 4 + 2 * p + 2)
                eng.wait_ge(send_loaded[p], i * 32 + 32)
                eng.sem_inc(pool_passed, 1)
                for k in range(2):
                    eng.indirect_dma_start(slots_d, bass.IndirectOffsetOnAxis(ap=send_at[:, p, k:k + 1], axis=0), send[:, p, k, :], None).then_inc(sent[p], 16)

            for p in range(2):
                dispatch(0, p)
            with eng.Fori(1, NTOK // 2) as i:
                for p in range(2):
                    dispatch(i, p)

            def expert_tile(j, q):
                p = q % 2
                e = eng.value_load(expert[0:1, bass.ds(j, 1)], min_val=0, max_val=NE - 1)
                eng.wait_ge(evar_ready, j + 1)
                eng.tensor_tensor(ers[:, p:p + 1], eve[:, p:p + 1], neg_half[:, 0:1], ALU.pow).then_inc(epow, 1)
                eng.wait_ge(epow, j + 1)
                eng.tensor_tensor(erw[:, p:p + 1], ers[:, p:p + 1], got[:, q, D + 1:D + 2], ALU.mult).then_inc(erw_ready, 1)
                eng.wait_ge(yn_ready, j + 1)
                eng.tensor_tensor(yg[:, p, :], yn[:, p, :], gb[:, 0, bass.ds(e, 1), :].rearrange("p o d -> p (o d)"), ALU.mult).then_inc(yg_ready, 1)
                eng.wait_ge(yo_ready, j + 1)
                eng.wait_ge(id_ready, j + 1)
                wait_past(eng, added[1 - p], (j + p) * 8)
                eng.sem_inc(pool_passed, 1)
                eng.indirect_dma_start(acc_d, bass.IndirectOffsetOnAxis(ap=got_id[:, p:p + 1], axis=0), yo[:, p, :], None,
                                       bounds_check=NTOKENS - 1, oob_is_err=False, compute_op=ALU.add).then_inc(added[p], 16)

            eng.wait_ge(expert_ready, 1)
            eng.wait_ge(w2_loaded, 48)
            for q in range(4):
                expert_tile(q, q)
            with eng.Fori(1, NSLOT // 4) as jj:
                for q in range(4):
                    expert_tile(jj * 4 + q, q)
            for g in range(NG):
                eng.wait_ge(f_var, g + 1)
                eng.tensor_tensor(frs[:, :], fve[:, :], neg_half[:, :], ALU.pow).then_inc(f_rstd, 1)
                eng.wait_ge(f_n, g + 1)
                if g >= 2:
                    eng.wait_ge(f_stored[g % 2], 16 * (g // 2))
                eng.tensor_tensor(fo[:, g % 2, :, :], fn[:, g % 2, :, :], fx1[:, g % 2, :, :], ALU.add).then_inc(f_o, 1)

        @block.scalar
        def _(eng):
            eng.wait_ge(w_loaded, 16 * 15)
            eng.wait_ge(dve_consts, 2)

            def a_xn(a):
                wait_for(eng, xt_t, 1, a, 1)
                wait_for(eng, xn_lo_ready, 1, a, 1, ago=1)
                eng.activation(xn[:, :], pA[:, 0, :], ACT.Identity, scale=nw[:, 0:1], bias=nb[:, 0:1]).then_inc(xn_ready, 1)
                wait_for(eng, ip_mm, 4, a, 4, ago=1)
                eng.activation(xn_hi[:, :], pA[:, 0, :], ACT.Identity, scale=nw[:, 0:1], bias=nb[:, 0:1]).then_inc(xn_ready, 1)

            def a_xi(a, f):
                wait_for(eng, ip_mm, 4, a, f + 1)
                wait_for(eng, cv_mm, 2, a, 2, ago=1)
                eng.activation(xi_hi[:, f, TAPS - 1:TAPS - 1 + SEQ], pA[:, 1 - f, :], ACT.Copy).then_inc(xi_hi_ready, 1)

            def a_z(a, f):
                wait_for(eng, ip_mm, 4, a, f + 3)
                wait_for(eng, yz_ready, 1, a, 1, ago=2)
                eng.activation(zs[:, a.parity, f, :], pA[:, 1 - f, :], ACT.Silu).then_inc(z_ready, 1)

            def a_u(a, f):
                wait_for(eng, cv_mm, 2, a, f + 1)
                wait_for(eng, rt_t, 6, a, 1, ago=2)
                wait_for(eng, r_odd_ready, 1, a, 1, ago=2)
                wait_for(eng, r_ready, 4, a, 1, ago=2)
                eng.activation(u[:, a.parity, f, :], pA[:, 1 - f, :], ACT.Silu, bias=cbias[:, f:f + 1]).then_inc(u_ready, 1)

            def a_xs(a):
                wait_for(eng, xs_mm, 1, a, 1)
                wait_for(eng, bc_ready, 1, a, 1, ago=2)
                wait_for(eng, ds_t, 1, a, 1, ago=2)
                eng.activation(xs[:, a.parity, :, :], pA[:, 1, 0:NT4 * 33].rearrange("p (t f) -> p t f", f=33), ACT.Copy).then_inc(xs_ready, 1)

            def b_rt(b, k):
                wait_for(eng, rt_t, 6, b, k + 1)
                if k < 2:
                    wait_for(eng, y_mm, 7, b, 5 + k, ago=1)
                else:
                    wait_for(eng, y_mm, 7, b, {2: 2, 3: 3, 4: 4}[k])
                eng.activation(RT[:, k % 2, :], pR[:, :, :].rearrange("p a b -> p (a b)"), ACT.Copy).then_inc(rt_ready, 1)

            def unit(a, b, c):
                if b is not None:
                    wait_for(eng, ds_t, 1, b, 1)
                    wait_for(eng, r_ready, 4, b, 1, ago=1)
                    wait_for(eng, dec_ready, 4, b, 1, ago=1)
                    wait_for(eng, pre_ready, 1, b, 1, ago=1)
                    for f in range(2):
                        i = eng.activation(dec1[:, f, :], pY[:, 0, :], ACT.Sigmoid, scale=ndtw[:, f:f + 1], bias=ndtb[:, f:f + 1])
                    i.then_inc(dec1_ready, 1)
                    wait_for(eng, bc_t, 1, b, 1)
                    wait_for(eng, y_mm, 7, b, 7, ago=1)
                    eng.activation(BCT[:, :, :], pB[:, :, :], ACT.Copy).then_inc(bct_ready, 1)
                    b_rt(b, 0)
                    wait_for(eng, rt_t, 6, b, 5, ago=1)
                    eng.activation(halves(R[:, :, :], 1)[:, :, 1:2], halves(u[:, b.parity, :, :], 1)[:, :, 1:2], ACT.Copy).then_inc(r_odd_ready, 1)
                    wait_for(eng, dec1_ready, 1, b, 1)
                    wait_for(eng, y_read, 5, b, 5, ago=1)
                    eng.activation(pre[:, :, :], dec1[:, :, :], ACT.Copy).then_inc(pre_ready, 1)
                if a is not None:
                    a_xn(a)
                if b is not None:
                    wait_for(eng, y_mm, 7, b, 1)
                    wait_for(eng, op_mm, 1, b, 1, ago=1)
                    eng.activation(y[:, :, :], pY[:, :, :], ACT.Copy).then_inc(y0_ready, 1)
                if a is not None:
                    a_xi(a, 0)
                    a_xi(a, 1)
                if b is not None:
                    b_rt(b, 1)
                if a is not None:
                    a_z(a, 0)
                    a_z(a, 1)
                if b is not None:
                    b_rt(b, 2)
                    b_rt(b, 3)
                if c is not None:
                    wait_for(eng, xf_t, 1, c, 1)
                    wait_for(eng, lg_mm, 1, c, 1, ago=1)
                    eng.activation(xfT[:, :], pB[:, 1, :], ACT.Copy).then_inc(xft_ready, 1)
                if b is not None:
                    b_rt(b, 4)
                    wait_for(eng, dec_ready, 4, b, 4)
                    wait_for(eng, hs_ready, 1, b, 1, ago=1)
                    eng.activation(decS[:, :, :, 1:NBLK],
                                   dec16[:, :, 1:NBLK].rearrange("p m (o b) -> p m o b", o=1).broadcast_to([P, 2, NST, NBLK - 1]),
                                   ACT.Copy).then_inc(decs_ready, 1)
                    wait_for(eng, y_mm, 7, b, 5)
                    for m in range(2):
                        i = eng.activation(Sall[:, m, :, :].rearrange("p s (t c) -> p t s c", t=NT4), pY[:, m, :].rearrange("p (t s c) -> p t s c", t=NT4, s=NST), ACT.Copy)
                    i.then_inc(s_ready, 1)
                if a is not None:
                    a_u(a, 0)
                if b is not None:
                    wait_for(eng, hs_ready, 1, b, 1)
                    wait_for(eng, rt_t, 6, b, 6, ago=1)
                    for m in range(2):
                        i = eng.activation(Hp[:, m, :, :].rearrange("p t (s c) -> p t s c", s=NST),
                                           Hs[:, m * NST * NBLK:(m + 1) * NST * NBLK].rearrange("p (s t c) -> p t s c", s=NST, t=NT4), ACT.Copy)
                    i.then_inc(hp_ready, 1)
                    wait_for(eng, rt_t, 6, b, 6)
                    wait_for(eng, y_mm, 7, b, 7, ago=1)
                    eng.activation(HT[:, :], pR[:, :, :].rearrange("p a b -> p (a b)"), ACT.Copy).then_inc(rt_ready, 1)
                if a is not None:
                    a_u(a, 1)
                    a_xs(a)

            run_units(eng, NS, unit)
            eng.wait_ge(xs_ready, NS)
            eng.wait_ge(rt_ready, 6 * NS)
            eng.wait_ge(xft_ready, NS)
            eng.nop().then_inc(stage1_act, 1)

            eng.wait_ge(gap_ready, 1)
            eng.activation(meta[:, :, 0, 1:2].rearrange("p t o -> p (t o)"), gap[:, :], ACT.Sigmoid).then_inc(weights_ready, 1)
            eng.activation(meta[:, :, 1, 1:2].rearrange("p t o -> p (t o)"), gap[:, :], ACT.Sigmoid, scale=-1.0).then_inc(weights_ready, 1)

            def xst(j, p):
                eng.wait_ge(xs_t, j + 1)
                eng.activation(xsT[:, p, :], pB[:, 0, 0:P], ACT.Copy).then_inc(xst_ready, 1)

            def silu(j, p):
                eng.wait_ge(h1_mm, j + 1)
                wait_past(eng, hid_ready, j - 1)
                eng.activation(sil[:, p, :], pA[:, p, :], ACT.Silu).then_inc(sil_ready, 1)

            def hidt(j, p):
                eng.wait_ge(h_t, j + 1)
                eng.activation(hidT[:, p, :], pY[:, p, :], ACT.Copy).then_inc(hidt_ready, 1)

            def tile_j(j, q, first=False, last=False):
                p = q % 2
                silu(j, p)
                if not first:
                    hidt(j - 1, 1 - p)
                if not last:
                    xst(j + 1, 1 - p)

            xst(0, 0)
            for q in range(4):
                tile_j(q, q, first=q == 0)
            with eng.Fori(1, NSLOT // 4 - 1) as jj:
                for q in range(4):
                    tile_j(jj * 4 + q, q)
            for q in range(4):
                tile_j(NSLOT - 4 + q, q, last=q == 3)
            hidt(NSLOT - 1, 1)


        @block.vector
        def _(eng):
            eng.wait_ge(w_loaded, 16 * 15)
            eng.tensor_scalar(ndtw[:, :], dtw[:, :], -1.0, None, ALU.mult).then_inc(dve_consts, 1)
            eng.tensor_scalar(ndtb[:, :], dtb[:, :], -1.0, None, ALU.mult).then_inc(dve_consts, 1)
            eng.wait_ge(e_loaded, 16 * 4)
            eng.tensor_copy(lower_b[:, :], lower_f[:, :]).then_inc(lower_ready, 1)
            eng.memset(ones_b[:, :], 1.0).then_inc(lower_ready, 1)
            eng.wait_ge(in_w_loaded, 16)
            eng.tensor_copy(in_hi[:, :], raw_w[:, 0:4 * P]).then_inc(w_hi, 1)
            eng.wait_ge(w_hi, 1)
            eng.tensor_tensor(in_lo[:, :], raw_w[:, 0:4 * P], in_hi[:, :].bitcast(fp32), ALU.subtract).then_inc(w_split, 1)
            eng.wait_ge(conv_w_loaded, 16)
            flat = lambda t: t[:, :, :, :].rearrange("p m k f -> p (m k f)")
            eng.tensor_copy(flat(conv_hi), raw_w[:, :]).then_inc(w_hi, 1)
            eng.wait_ge(w_hi, 2)
            eng.tensor_tensor(flat(conv_lo), raw_w[:, :], flat(conv_hi).bitcast(fp32), ALU.subtract).then_inc(w_split, 1)

            def norm_stats(chain, seq, src, mv, ve, done):
                for t in range(NT4):
                    chain.link(eng.bn_stats(stats[:, t, :], src[:, t, :]))
                chain.wait()
                eng.sem_inc(dve_passed, 1)
                for t in range(NT4):
                    chain.link(eng.bn_aggr(mv[:, t, :], stats[:, t, :]))
                chain.wait()
                eng.tensor_scalar(ve[:, :], mv[:, :, 1:2].rearrange("p t o -> p (t o)"), EPS, None, ALU.add).then_inc(done, 1)

            def norm_apply(seq, k, dst, src, mv, rs, rstd, done):
                wait_for(eng, rstd, 2, seq, k)
                for t in range(NT4):
                    i = eng.tensor_scalar(dst[:, t, :], src[:, t, :], mv[:, t, 0:1], rs[:, t:t + 1], ALU.subtract, ALU.mult)
                i.then_inc(done, 1)

            def level(chain, b, n):
                h = HALVES[n]
                half = tmp[:, 0, :].rearrange("p (b k) -> p b k", k=h)
                wait_for(eng, y_mm, 7, b, (2, 3, 4, 6)[n])
                eng.tensor_tensor(half, halves(pY[:, :, :], h)[:, :, h:2 * h], halves(pre[:, :, :], h)[:, :, h:2 * h], ALU.mult).then_inc(y_read, 1)
                wait_for(eng, y_read, 5, b, n + 1)
                yr = halves(y[:, :, :], h)[:, :, h:2 * h]
                chain.link(eng.tensor_tensor(yr, yr, half, ALU.add))
                pr = halves(pre[:, :, :], h)
                chain.step(eng.tensor_tensor(pr[:, :, h:2 * h], pr[:, :, h:2 * h], pr[:, :, h - 1:h].broadcast_to([P, SEQ // h, h]), ALU.mult))

            def unit(a, b, c):
                ca, cb, cc = (Chain(eng, q, n, seq) for q, n, seq in ((dve_a, 16, a), (dve_b, 10, b), (dve_c, 26, c)))
                if b is not None:
                    wait_for(eng, xs_ready, 1, b, 1)
                    wait_for(eng, bc_t, 1, b, 1, ago=1)
                    wait_for(eng, y_mm, 7, b, 5, ago=1)
                    for k in range(2):
                        i = eng.tensor_tensor(BC[:, k, :, :].rearrange("p t (s c) -> p t s c", s=NST),
                                              xs[:, b.parity, :, 1 + k * NST:1 + (k + 1) * NST].rearrange("p t (s o) -> p t s o", o=1).broadcast_to([P, NT4, NST, CB]),
                                              block_mask[:, :].rearrange("p (a o c) -> p a o c", a=1, o=1).broadcast_to([P, NT4, NST, CB]), ALU.mult)
                    i.then_inc(bc_ready, 1)
                if a is not None:
                    eng.wait_ge(x_loaded[a.parity], a.half * 16 + 16)
                    norm_stats(ca, a, xin[:, a.parity, :, :], mv1, ve1, var_a)
                if c is not None:
                    wait_for(eng, at_ready, 1, c, 1)
                    norm_stats(cc, c, at, mv3, ve3, var_c)
                if a is not None:
                    wait_for(eng, at_ready, 1, a, 1, ago=2)
                    norm_apply(a, 1, xa[:, a.parity, :, :], xin[:, a.parity, :, :], mv1, rs1, rstd_a, xa_ready)
                    wait_for(eng, xa_ready, 1, a, 1)
                    wait_for(eng, xb_ready, 1, a, 1, ago=1)
                    norm_stats(ca, a, xa[:, a.parity, :, :], mv2, ve2, var_a)
                    ca.end()
                if b is not None:
                    wait_for(eng, g_mm, 1, b, 1)
                    wait_for(eng, y_mm, 7, b, 6, ago=1)
                    for n in range(5):
                        i = eng.tensor_tensor(G[:, n, :].rearrange("p (t r) -> p t r", t=NT4), pB[:, 0, :].rearrange("p (t r) -> p t r", t=NT4),
                                              level_mask[:, n:n + 1, :].broadcast_to([P, NT4, P]), ALU.mult)
                    i.then_inc(g_ready, 1)
                if c is not None:
                    wait_for(eng, x1_ready, 1, c, 1, ago=1)
                    norm_apply(c, 1, x1n, at, mv3, rs3, rstd_c, x1n_ready)
                if a is not None:
                    wait_for(eng, xt_t, 1, a, 1, ago=1)
                    norm_apply(a, 2, xb, xa[:, a.parity, :, :], mv2, rs2, rstd_a, xb_ready)
                if b is not None:
                    wait_for(eng, y0_ready, 1, b, 1)
                    wait_for(eng, pre_ready, 1, b, 1)
                    level(cb, b, 0)
                if a is not None:
                    for f in range(2):
                        wait_for(eng, xi_hi_ready, 2, a, f + 1)
                        wait_for(eng, cv_mm, 2, a, 2, ago=1)
                        w = slice(TAPS - 1, TAPS - 1 + SEQ)
                        eng.tensor_tensor(xi_lo[:, f, w], pA[:, 1 - f, :], xi_hi[:, f, w].bitcast(fp32), ALU.subtract).then_inc(xi_lo_ready, 1)
                if c is not None:
                    wait_for(eng, x1_ready, 1, c, 1)
                    wait_for(eng, xf_ready, 1, c, 1, ago=1)
                    norm_stats(cc, c, x1, mv4, ve4, var_c)
                if b is not None:
                    level(cb, b, 1)
                if c is not None:
                    wait_for(eng, xf_t, 1, c, 1, ago=1)
                    wait_for(eng, xf_stored, 16, c, 16, ago=1)
                    norm_apply(c, 2, xf, x1, mv4, rs4, rstd_c, xf_ready)
                if b is not None:
                    level(cb, b, 2)
                    wait_for(eng, s_ready, 1, b, 1)
                    wait_for(eng, decs_ready, 1, b, 1)
                    wait_for(eng, hp_ready, 1, b, 1, ago=1)
                    cb.step(eng.tensor_tensor_scan(Hs[:, 1:1 + 2 * NST * NBLK], decS[:, :, :, :].rearrange("p m s b -> p (m s b)"),
                                                   Sall[:, :, :, :].rearrange("p m s b -> p (m s b)"), 0.0, ALU.mult, ALU.add))
                    eng.memset(Hs[:, 0:2 * NST * NBLK].rearrange("p (r b) -> p r b", b=NBLK)[:, :, 0:1], 0.0).then_inc(hs_ready, 1)
                if c is not None:
                    wait_for(eng, lg_mm, 1, c, 1)
                    eng.tensor_tensor(lg[:, :, :], pB[:, 1, 0:NT4 * NE].rearrange("p (t e) -> p t e", e=NE),
                                      brb[:, :].rearrange("p (o e) -> p o e", o=1).broadcast_to([P, NT4, NE]), ALU.add).then_inc(lg_read, 1)
                    wait_for(eng, lg_read, 1, c, 1)
                    eng.sem_inc(dve_passed, 1)
                    for t in range(NT4):
                        cc.link(eng.max(top8[:, t, :], lg[:, t, :]))
                    cc.wait()
                    eng.sem_inc(dve_passed, 1)
                    for t in range(NT4):
                        cc.link(eng.max_index(topi8[:, t, :], top8[:, t, :], lg[:, t, :]))
                    cc.wait()
                    cc.link(eng.tensor_copy(top[:, bass.ds(c.s * NT4, NT4), :], top8[:, :, 0:2]))
                    cc.step(eng.tensor_copy(topi[:, bass.ds(c.s * NT4, NT4), :], topi8[:, :, 0:2]))
                    cc.end()
                if b is not None:
                    level(cb, b, 3)
                    wait_for(eng, y_mm, 7, b, 7)
                    eng.tensor_tensor(tmp[:, :, :], pY[:, :, :], pre[:, :, :], ALU.mult).then_inc(y_read, 1)
                    wait_for(eng, y_read, 5, b, 5)
                    cb.step(eng.tensor_tensor(y[:, :, :], y[:, :, :], tmp[:, :, :], ALU.add))
                    cb.end()
                    wait_for(eng, z_ready, 2, b, 2)
                    eng.tensor_tensor(y[:, :, :], y[:, :, :], zs[:, b.parity, :, :], ALU.mult).then_inc(yz_ready, 1)
                    wait_for(eng, op_mm, 1, b, 1)
                    wait_for(eng, x1n_ready, 1, b, 1, ago=1)
                    eng.tensor_tensor(at[:, :, :], pB[:, 0, :].rearrange("p (t d) -> p t d", t=NT4), xa[:, b.parity, :, :], ALU.add).then_inc(at_ready, 1)

            run_units(eng, NS, unit)
            eng.wait_ge(at_ready, NS)
            eng.wait_ge(xf_ready, NS)
            eng.wait_ge(yz_ready, NS)
            eng.nop().then_inc(stage1_dve, 1)

            for q in (stage1_pe, stage1_act, stage1_pool, stage1_sp):
                eng.wait_ge(q, 1)
            r = Chain(eng, route, 0, Seq(0, 0, 0))
            r.link(eng.memset(reset[:, :, :], 1.0))
            r.link(eng.memset(ones_e[:, :], 1.0))
            for k in range(2):
                i = eng.tensor_copy(meta[:, :, k, 0:1].rearrange("p t o -> p (t o)"), tokid[:, :])
            i.then_inc(weights_ready, 1)
            eng.tensor_tensor(gap[:, :], top[:, :, 0:1].rearrange("p t o -> p (t o)"), top[:, :, 1:2].rearrange("p t o -> p (t o)"), ALU.subtract).then_inc(gap_ready, 1)
            ev = iota_es[:, :].rearrange("p (o e) -> p o e", o=1).broadcast_to([P, NTOK, NE])
            for k, m in enumerate((m1, m2)):
                r.link(eng.tensor_tensor(m[:, :, :], ev, topi[:, :, k:k + 1].broadcast_to([P, NTOK, NE]), ALU.is_equal))
            r.wait()
            eng.tensor_tensor(m12[:, :].rearrange("p (t e) -> p t e", e=NE), m1[:, :, :], m2[:, :, :], ALU.add).then_inc(m12_ready, 1)
            r.step(eng.memset(reset[:, :, 0:1], 0.0))
            eng.wait_ge(rank_mm, 2)
            flat2 = lambda t: t[:, :, :].rearrange("p a b -> p (a b)")
            pTot = pR[:, :, :].rearrange("p a b -> p (a b)")[:, 0:NTOK * NE]
            pRank = pY[:, :, :].rearrange("p a b -> p (a b)")[:, 0:NTOK * NE]
            r.step(eng.tensor_copy(totals[:, :, :], pTot.rearrange("p (t e) -> p e t", e=NE)))
            r.step(eng.tensor_tensor_scan(flat2(seen), flat2(reset), flat2(totals), 0.0, ALU.mult, ALU.add))
            r.step(eng.tensor_scalar(count_i[:, :], seen[:, :, NTOK - 1:NTOK].rearrange("p e o -> p (e o)"), float(P - 1), None, ALU.add))
            r.step(eng.tensor_scalar(ntiles_i[:, :], count_i[:, :], 7, None, ALU.arith_shift_right))
            r.step(eng.tensor_copy(ntiles[:, :], ntiles_i[:, :]))
            r.step(eng.tensor_tensor_scan(tiles_to[:, :], ones_e[:, :], ntiles[:, :], 0.0, ALU.mult, ALU.add))
            r.step(eng.tensor_tensor(base[:, :], tiles_to[:, :], ntiles[:, :], ALU.subtract))
            r.step(eng.tensor_scalar(base[:, :], base[:, :], float(P), None, ALU.mult))
            r.step(eng.tensor_tensor(seen[:, :, :], seen[:, :, :], totals[:, :, :], ALU.subtract))
            r.step(eng.tensor_tensor(seen[:, :, :], seen[:, :, :], base[:, :].rearrange("p (e o) -> p e o", o=1).broadcast_to([P, NE, NTOK]), ALU.add))
            r.step(eng.tensor_tensor(place[:, :, :], seen[:, :, :].rearrange("p e t -> p t e"), pRank.rearrange("p (t e) -> p t e", e=NE), ALU.add))
            for m in (m1, m2):
                r.link(eng.tensor_tensor(m[:, :, :], m[:, :, :], place[:, :, :], ALU.mult))
            r.wait()
            for k, m in enumerate((m1, m2)):
                eng.tensor_reduce(pos[:, :, k:k + 1].rearrange("p t o -> p (t o)"), m[:, :, :], AX.X, ALU.add).then_inc(pos_ready, 1)
            eng.wait_ge(pos_ready, 2)
            for n in range(0, NSLOT, NTOK):
                w = min(NTOK, NSLOT - n)
                r.step(eng.tensor_tensor(m1[0:1, 0:w, :], iota_ts[:, n:n + w].rearrange("p (t o) -> p t o", o=1).broadcast_to([1, w, NE]),
                                         tiles_to[0:1, :].rearrange("p (o e) -> p o e", o=1).broadcast_to([1, w, NE]), ALU.is_ge))
                r.step(eng.tensor_reduce(expert_f[:, n:n + w], m1[0:1, 0:w, :], AX.X, ALU.add))
            eng.tensor_scalar(expert[:, :], expert_f[:, :], float(NE - 1), None, ALU.min).then_inc(expert_ready, 1)

            def mult(j, p):
                eng.wait_ge(sil_ready, j + 1)
                eng.wait_ge(h3_mm, j + 1)
                wait_past(eng, h_t, j - 1)
                eng.tensor_tensor(hid[:, p, :], pR[:, p, :], sil[:, p, :], ALU.mult).then_inc(hid_ready, 1)

            def finish(j, q):
                p = q % 2
                eng.wait_ge(yo_mm, j + 1)
                c = Chain(eng, est_c, 2, Seq(j, 0, 0))
                c.step(eng.bn_stats(est[:, :], pB[:, 1, 0:D]))
                eng.sem_inc(dve_passed, 1)
                c.step(eng.bn_aggr(emv[:, p, :], est[:, :]))
                eng.tensor_scalar(eve[:, p:p + 1], emv[:, p, 1:2], EPS, None, ALU.add).then_inc(evar_ready, 1)
                wait_past(eng, added[p], (j - p) * 8)
                eng.wait_ge(got_loaded[q], (j - q) * 4 + 16)
                eng.tensor_copy(got_id[:, p:p + 1], got[:, q, D:D + 1]).then_inc(id_ready, 1)
                eng.wait_ge(erw_ready, j + 1)
                wait_past(eng, yg_ready, j - 1)
                eng.tensor_scalar(yn[:, p, :], pB[:, 1, 0:D], emv[:, p, 0:1], erw[:, p:p + 1], ALU.subtract, ALU.mult).then_inc(yn_ready, 1)

            def weigh(j, q):
                p = q % 2
                e = eng.value_load(expert[0:1, bass.ds(j, 1)], min_val=0, max_val=NE - 1)
                eng.wait_ge(yg_ready, j + 1)
                eng.scalar_tensor_tensor(out=yo[:, p, :], in0=gb[:, 1, bass.ds(e, 1), :].rearrange("p o d -> p (o d)"), scalar=got[:, q, D + 1:D + 2], in1=yg[:, p, :],
                                         op0=ALU.mult, op1=ALU.add).then_inc(yo_ready, 1)

            eng.wait_ge(expert_ready, 1)
            eng.wait_ge(w2_loaded, 48)

            def tile_j(j, q, first=False):
                mult(j, q % 2)
                if not first:
                    finish(j - 1, (q - 1) % 4)
                    weigh(j - 1, (q - 1) % 4)

            for q in range(4):
                tile_j(q, q, first=q == 0)
            with eng.Fori(1, NSLOT // 4) as jj:
                for q in range(4):
                    tile_j(jj * 4 + q, q)
            finish(NSLOT - 1, 3)
            weigh(NSLOT - 1, 3)

            for g in range(NG):
                c = Chain(eng, f_chain, 8, Seq(g, 0, 0))
                eng.wait_ge(f_loaded[g % 2], 32 * (g // 2 + 1))
                for t in range(NT4):
                    c.link(eng.bn_stats(fst[:, t, :], facc[:, g % 2, t, :]))
                c.wait()
                for t in range(NT4):
                    c.link(eng.bn_aggr(fmv[:, t, :], fst[:, t, :]))
                c.wait()
                eng.tensor_scalar(fve[:, :], fmv[:, :, 1:2].rearrange("p t o -> p (t o)"), EPS, None, ALU.add).then_inc(f_var, 1)
                eng.wait_ge(f_rstd, g + 1)
                if g >= 2:
                    eng.wait_ge(f_o, g - 1)
                for t in range(NT4):
                    i = eng.tensor_scalar(fn[:, g % 2, t, :], facc[:, g % 2, t, :], fmv[:, t, 0:1], frs[:, t:t + 1], ALU.subtract, ALU.mult)
                i.then_inc(f_n, 1)

        @block.tensor
        def _(eng):
            eng.wait_ge(w_loaded, 16 * 15)
            eng.wait_ge(w_split, 2)
            eng.wait_ge(const_ready, 5)

            def tile(t):
                return slice(t * P, (t + 1) * P)

            def split_mm(out, hi, lo, x_hi, x_lo, start, stop):
                eng.matmul(out, hi, x_hi, start=start, stop=False)
                eng.matmul(out, hi, x_lo, start=False, stop=False)
                return eng.matmul(out, lo, x_hi, start=False, stop=stop)

            def b_rt(b, k, src):
                if k:
                    wait_for(eng, rt_ready, 6, b, k)
                else:
                    wait_for(eng, rt_ready, 6, b, 6, ago=1)
                for t in range(NT4):
                    for m in range(2):
                        i = eng.transpose(pR[:, t // 2, (t % 2) * DI + m * P:(t % 2) * DI + (m + 1) * P], src(m, t), ident[:, :])
                i.then_inc(rt_t, 1)

            def b_y(b, k, n, free):
                wait_for(eng, rt_ready, 6, b, k + 1)
                free()
                for m in range(2):
                    for t in range(NT4):
                        i = eng.matmul(pY[:, m, tile(t)], RT[:, k % 2, t * DI + m * P:t * DI + (m + 1) * P], G[:, n, tile(t)], start=True, stop=True)
                i.then_inc(y_mm, 1)

            def a_in(a, f):
                if f == 0:
                    wait_for(eng, xn_lo_ready, 1, a, 1)
                    wait_for(eng, xs_ready, 1, a, 1, ago=1)
                elif f > 1:
                    wait_for(eng, xi_hi_ready, 2, a, f - 1)
                    wait_for(eng, xi_lo_ready, 2, a, f - 1)
                split_mm(pA[:, 1 - f % 2, :], in_hi[:, tile(f)], in_lo[:, tile(f)], xn_hi[:, :], xn_lo[:, :], True, True).then_inc(ip_mm, 1)

            def a_conv(a, f, part):
                if part == 0:
                    wait_for(eng, z_ready, 2, a, f + 1)
                for k in range(TAPS):
                    w = slice(k, k + SEQ)
                    i = split_mm(pA[:, 1 - f, :], conv_hi[:, part, k, tile(f)], conv_lo[:, part, k, tile(f)], xi_hi[:, part, w], xi_lo[:, part, w],
                                 part == 0 and k == 0, part == 1 and k == TAPS - 1)
                if part:
                    i.then_inc(cv_mm, 1)

            def unit(a, b, c):
                if b is not None:
                    wait_for(eng, xs_ready, 1, b, 1)
                    wait_for(eng, y_read, 5, b, 5, ago=1)
                    for t in range(NT4):
                        i = eng.transpose(pY[:, 0, tile(t)], xs[:, b.parity, t, 0:1].broadcast_to([P, P]), ident[:, :])
                    i.then_inc(ds_t, 1)
                    wait_for(eng, bc_ready, 1, b, 1)
                    wait_for(eng, at_ready, 1, b, 1, ago=1)
                    if c is not None:
                        wait_for(eng, lg_read, 1, c, 1, ago=1)
                    for k in range(2):
                        for t in range(NT4):
                            i = eng.transpose(pB[:, k, tile(t)], BC[:, k, t, :], ident[:, :])
                    i.then_inc(bc_t, 1)
                    wait_for(eng, u_ready, 2, b, 2)
                    b_rt(b, 0, lambda m, t: u[:, b.parity, m, tile(t)])
                    wait_for(eng, bct_ready, 1, b, 1)
                    for t in range(NT4):
                        i = eng.matmul(pB[:, 0, tile(t)], BCT[:, 0, tile(t)], BCT[:, 1, tile(t)], start=True, stop=True)
                    i.then_inc(g_mm, 1)
                if a is not None:
                    wait_for(eng, xb_ready, 1, a, 1)
                    wait_for(eng, u_ready, 2, a, 2, ago=1)
                    for t in range(NT4):
                        i = eng.transpose(pA[:, 0, tile(t)], xb[:, t, :], ident[:, :])
                    i.then_inc(xt_t, 1)
                if b is not None:
                    wait_for(eng, g_ready, 1, b, 1)
                    b_y(b, 0, 4, lambda: wait_for(eng, dec1_ready, 1, b, 1))
                if a is not None:
                    a_in(a, 0)
                    a_in(a, 1)
                src = lambda m, t: R[:, m, tile(t)]
                if b is not None:
                    wait_for(eng, r_ready, 4, b, 1)
                    wait_for(eng, r_odd_ready, 1, b, 1)
                    b_rt(b, 1, src)
                    b_y(b, 0, 0, lambda: wait_for(eng, y0_ready, 1, b, 1))
                if a is not None:
                    a_in(a, 2)
                    a_in(a, 3)
                if b is not None:
                    wait_for(eng, r_ready, 4, b, 2)
                    b_rt(b, 2, src)
                    b_y(b, 1, 1, lambda: wait_for(eng, y_read, 5, b, 1))
                if a is not None:
                    a_conv(a, 0, 0)
                if b is not None:
                    wait_for(eng, r_ready, 4, b, 3)
                    b_rt(b, 3, src)
                    b_y(b, 2, 2, lambda: wait_for(eng, y_read, 5, b, 2))
                if c is not None:
                    wait_for(eng, xf_ready, 1, c, 1)
                    if b is not None:
                        wait_for(eng, bct_ready, 1, b, 1)
                    else:
                        wait_for(eng, lg_read, 1, c, 1, ago=1)
                    for t in range(NT4):
                        i = eng.transpose(pB[:, 1, tile(t)], xf[:, t, :], ident[:, :])
                    i.then_inc(xf_t, 1)
                if a is not None:
                    a_conv(a, 0, 1)
                if b is not None:
                    wait_for(eng, r_ready, 4, b, 4)
                    b_rt(b, 4, src)
                    wait_for(eng, rt_ready, 6, b, 5)
                    wait_for(eng, y_read, 5, b, 3)
                    for m in range(2):
                        for t in range(NT4):
                            i = eng.matmul(pY[:, m, tile(t)], RT[:, 0, t * DI + m * P:t * DI + (m + 1) * P], BC[:, 0, t, :], start=True, stop=True)
                    i.then_inc(y_mm, 1)
                if a is not None:
                    a_conv(a, 1, 0)
                if c is not None:
                    wait_for(eng, xft_ready, 1, c, 1)
                    for t in range(NT4):
                        i = eng.matmul(pB[:, 1, t * NE:(t + 1) * NE], xfT[:, tile(t)], wr_sb[:, :], start=True, stop=True)
                    i.then_inc(lg_mm, 1)
                if b is not None:
                    b_y(b, 3, 3, lambda: wait_for(eng, s_ready, 1, b, 1))
                if a is not None:
                    a_conv(a, 1, 1)
                if b is not None:
                    wait_for(eng, hp_ready, 1, b, 1)
                    b_rt(b, 5, lambda m, t: Hp[:, m, t, :])
                    wait_for(eng, rt_ready, 6, b, 6)
                    wait_for(eng, y_read, 5, b, 4)
                    for m in range(2):
                        for t in range(NT4):
                            i = eng.matmul(pY[:, m, tile(t)], HT[:, t * DI + m * P:t * DI + (m + 1) * P], BCT[:, 1, tile(t)], start=True, stop=True)
                    i.then_inc(y_mm, 1)
                if a is not None:
                    wait_for(eng, u_ready, 2, a, 2)
                    for t in range(NT4):
                        for m in range(2):
                            i = eng.matmul(pA[:, 1, t * 33:(t + 1) * 33], u[:, a.parity, m, tile(t)], xproj[:, m, :], start=m == 0, stop=m == 1)
                    i.then_inc(xs_mm, 1)
                if b is not None:
                    wait_for(eng, yz_ready, 1, b, 1)
                    for t in range(NT4):
                        for m in range(2):
                            i = eng.matmul(pB[:, 0, tile(t)], y[:, m, tile(t)], outproj[:, m, :], start=m == 0, stop=m == 1)
                    i.then_inc(op_mm, 1)

            run_units(eng, NS, unit)
            eng.wait_ge(op_mm, NS)
            eng.wait_ge(lg_mm, NS)
            eng.nop().then_inc(stage1_pe, 1)

            eng.wait_ge(lower_ready, 2)
            eng.wait_ge(m12_ready, 1)
            eng.wait_ge(s_ready, NS)
            for q, w in ((pR, ones_b), (pY, lower_b)):
                for h in range(0, NTOK * NE, SEQ):
                    i = eng.matmul(q[:, h // SEQ, 0:min(SEQ, NTOK * NE - h)], w[:, :], m12[:, h:min(h + SEQ, NTOK * NE)], start=True, stop=True)
                i.then_inc(rank_mm, 1)
            eng.wait_ge(pos_ready, 2)

            eng.wait_ge(w13_loaded, 16)
            eng.wait_ge(w2_loaded, 48)
            eng.wait_ge(expert_ready, 1)

            def x_t(j, q):
                eng.wait_ge(got_loaded[q], (j - q) * 4 + 16)
                wait_past(eng, xst_ready, j)
                eng.transpose(pB[:, 0, 0:P], got[:, q, 0:D], ident[:, :]).then_inc(xs_t, 1)

            def up(j, p, e, k, out, free, done):
                if k == 0:
                    eng.wait_ge(xst_ready, j + 1)
                wait_past(eng, free, j - 1)
                eng.matmul(out[:, p, :], xsT[:, p, :], w13_sb[:, bass.ds(e, 1), k, :].rearrange("p o f -> p (o f)"), start=True, stop=True).then_inc(done, 1)

            def hid_t(j, p):
                eng.wait_ge(hid_ready, j + 1)
                wait_past(eng, hidt_ready, j - 1)
                for c in range(FC):
                    i = eng.transpose(pY[:, p, tile(c)], hid[:, p, tile(c)], ident[:, :])
                i.then_inc(h_t, 1)

            def down(j, p, e):
                eng.wait_ge(hidt_ready, j + 1)
                wait_past(eng, yn_ready, j)
                for c in range(FC):
                    i = eng.matmul(pB[:, 1, 0:D], hidT[:, p, tile(c)], w2_sb[:, c, bass.ds(e, 1), :].rearrange("p o d -> p (o d)"), start=c == 0, stop=c == FC - 1)
                i.then_inc(yo_mm, 1)

            def tile_j(j, q, first=False, last=False):
                p = q % 2
                e = eng.value_load(expert[0:1, bass.ds(j, 1)], min_val=0, max_val=NE - 1)
                up(j, p, e, 0, pA, sil_ready, h1_mm)
                if not first:
                    hid_t(j - 1, 1 - p)
                up(j, p, e, 1, pR, hid_ready, h3_mm)
                if not first:
                    before = eng.value_load(expert[0:1, bass.ds(j - 1, 1)], min_val=0, max_val=NE - 1)
                    down(j - 1, 1 - p, before)
                if not last:
                    x_t(j + 1, (q + 1) % 4)

            x_t(0, 0)
            for q in range(4):
                tile_j(q, q, first=q == 0)
            with eng.Fori(1, NSLOT // 4 - 1) as jj:
                for q in range(4):
                    tile_j(jj * 4 + q, q)
            for q in range(4):
                tile_j(NSLOT - 4 + q, q, last=q == 3)
            hid_t(NSLOT - 1, 1)
            down(NSLOT - 1, 1, eng.value_load(expert[0:1, NSLOT - 1:NSLOT], min_val=0, max_val=NE - 1))


_INS = ['x', 'norm_w', 'norm_b', 'in_wT', 'conv_wT', 'conv_b', 'x_wT', 'dt_w', 'dt_b', 'out_wT', 'masks', 'blockmask', 'ident', 'br', 'wr', 'w13', 'w2', 'gamma', 'beta', 'lower', 'iota_e', 'iota_t', 'token_id']


def kernel(**inputs):
    import numpy as _np
    import concourse.bacc as _bacc
    from concourse import mybir as _mybir
    from concourse.bass_utils import run_bass_kernel_spmd as _run
    nc = _bacc.Bacc("TRN2", target_bir_lowering=False, num_devices=1)
    g = {k.replace('L0_attn_', '').replace('L0_ffn_', 'f_'): _np.asarray(v) for k, v in inputs.items()}
    r = _np.arange(128)
    masks = _np.stack([((r[:, None] // (2 * h) == r[None, :] // (2 * h)) & (r[:, None] % (2 * h) < h) & (r[None, :] % (2 * h) >= h)) for h in (1, 2, 4, 8)]
                      + [r[:, None] == r[None, :]], 1).astype(_np.float32)
    d = {'x': g['x'], 'norm_w': g['norm_w'], 'norm_b': g['norm_b'], 'in_wT': g['in_proj_w'].T,
         'conv_wT': g['conv_w'].reshape(256, 2, 128, 4).transpose(2, 1, 3, 0).reshape(128, -1), 'conv_b': g['conv_b'],
         'x_wT': g['x_proj_w'].T, 'dt_w': g['dt_w'], 'dt_b': g['dt_b'], 'out_wT': g['out_proj_w'].T,
         'masks': masks, 'blockmask': (r[:, None] // 16 == _np.arange(8)[None]).astype(_np.float32), 'ident': _np.eye(128, dtype=_np.float32),
         'br': g['f_br'], 'wr': g['f_Wr']}
    NS = g['x'].shape[0]
    nslot = (2 * NS * 512 + 16 * 127) // 128
    nslot += -nslot % 4
    d['w13'] = _np.stack([g['f_W1'], g['f_W3']], 1).transpose(2, 0, 1, 3)
    d['w2'] = g['f_W2'].reshape(16, 4, 128, 128).transpose(2, 1, 0, 3)
    d['gamma'], d['beta'] = g['f_gamma'], g['f_beta']
    d['lower'] = (r[:, None] < r[None, :]).astype(_np.float32)
    d['iota_e'] = _np.tile(_np.arange(16, dtype=_np.float32)[None], (128, 1))
    d['iota_t'] = _np.arange(nslot, dtype=_np.float32)[None]
    d['token_id'] = (r[:, None] + 128 * _np.arange(NS * 4)[None]).astype(_np.float32)
    _OUTS = [((NS, 512, 128), 'float32')]
    arrays, args = {}, []
    for name in _INS:
        a = _np.ascontiguousarray(d[name])
        arrays[f"in_{name}_dram"] = a
        args.append(nc.dram_tensor(f"in_{name}_dram", a.shape, _mybir.dt.from_np(a.dtype), kind="ExternalInput").ap())
    for i, (shape, dtype) in enumerate(_OUTS):
        args.append(nc.dram_tensor(f"out_{i}_dram", shape, _mybir.dt.from_np(_np.dtype(dtype)), kind="ExternalOutput").ap())
    sandwich(nc, NS, *args)
    r = _run(nc, [arrays], core_ids=[0])
    return r.results[0]["out_0_dram"]
```

```python
import numpy as np
import concourse.bass as bass
from concourse import mybir
from contextlib import ExitStack

P = 128
SEQ = 512
D = 128
DI = 256
NST = 16
TAPS = 4
NT4 = SEQ // P
Q = 16
NBLK = SEQ // Q
CB = P // Q
HALVES = (1, 2, 4, 8)
NE = 16
EPS = 1e-5
DF = 512
FC = DF // P
ROW = D + 2
NOWHERE = 1 << 20

fp32 = mybir.dt.float32
f32r = mybir.dt.float32r
i32 = mybir.dt.int32
u32 = mybir.dt.uint32
bf16 = mybir.dt.bfloat16
ALU = mybir.AluOpType
ACT = mybir.ActivationFunctionType
AX = mybir.AxisListType


class Seq:

    def __init__(self, s, half, parity):
        self.s, self.half, self.parity = s, half, parity


class Chain:

    def __init__(self, eng, sem, per, seq):
        self.eng, self.sem, self.at, self.per, self.seq = eng, sem, 0, per, seq

    def link(self, ins):
        self.at += 1
        ins.then_inc(self.sem, 1)

    def wait(self):
        self.eng.wait_ge(self.sem, self.seq.s * self.per + self.at)

    def step(self, ins):
        self.link(ins)
        self.wait()

    def end(self):
        assert self.at == self.per, (self.at, self.per)


def wait_for(eng, sem, per, seq, k, ago=0):
    n = seq.s - ago
    if isinstance(n, int) and n < 0:
        return
    eng.wait_ge(sem, n * per + k)


def wait_past(eng, sem, value):
    if not (isinstance(value, int) and value <= 0):
        eng.wait_ge(sem, value)


def run_units(eng, ns, unit):
    seq = lambda n: Seq(n, n // 2, n % 2) if 0 <= n < ns else None
    for k in range(4):
        unit(*(seq(k - n) for n in range(4)))
    with eng.Fori(0, ns // 2 - 2) as j:
        for p in range(2):
            unit(*(Seq(j * 2 + (4 + p - n), j + (4 + p - n) // 2, (p - n) % 2) for n in range(4)))
    for k in range(ns, ns + 3):
        unit(*(seq(k - n) for n in range(4)))


def sandwich(nc, NS, x, norm_w, norm_b, in_wT, conv_wT, conv_b, x_wT, dt_w, dt_b, out_wT, masks, blockmask, ident_d,
             br, wr, w13, w2, gamma, beta, lower, iota_e, iota_p, region, token_id, out):
    NTOK = NS * NT4
    NTOKENS = NTOK * P
    NSLOT = (2 * NTOKENS + NE * (P - 1)) // P
    NSLOT += -NSLOT % 4
    NG = NTOK // NT4
    x1_d = nc.dram_tensor("x1_scratch", [NTOKENS, D], fp32).ap()
    REGION = NTOKENS + P
    BLANK = NE * REGION
    slots_d = nc.dram_tensor("slots_scratch", [BLANK + P, ROW], fp32).ap()
    chosen_d = nc.dram_tensor("chosen_scratch", [2 * NTOKENS, D], fp32).ap()
    assert NSLOT <= 2 * P and BLANK + P < NOWHERE
    ctx = ExitStack()
    early = ExitStack()
    with ctx:
        def sb(name, shape, dt=fp32):
            return (early if in_early[0] else ctx).enter_context(nc.sbuf_tensor(name, shape, dt))

        in_early = [False]

        def pb(name, shape, dt=fp32):
            return ctx.enter_context(nc.psum_tensor(name, shape, dt))

        def sem(name):
            return ctx.enter_context(nc.semaphore(name))

        ident = sb("ident", [P, P])
        neg_half = sb("neg_half", [P, NT4])
        blank = sb("blank", [P, ROW])
        lower_b = sb("lower_b", [P, P], bf16)
        ones_b = sb("ones_b", [P, P], bf16)
        iota_es = sb("iota_es", [P, NE])
        slot_no = sb("slot_no", [P, 2])
        region_sb = sb("region_sb", [P, NE])
        running = sb("running", [P, NE])
        tokid = sb("tokid", [P, 2, NTOK])
        count_i = sb("count_i", [P, NE], i32)
        ntiles_i = sb("ntiles_i", [P, NE], i32)
        ntiles = sb("ntiles", [P, NE])
        tiles_to = sb("tiles_to", [P, NE])
        before = sb("before", [P, NE])
        shift = sb("shift", [P, NE])
        shift_step = sb("shift_step", [P, NE])
        ones_e = sb("ones_e", [P, NE])
        tail_at = sb("tail_at", [P, NE], i32)
        past = sb("past", [P, 2, NE])
        past_step = sb("past_step", [P, 2, NE])
        slot_cols = sb("slot_cols", [P, 4])
        slot_table = sb("slot_table", [1, 4 * P], i32)
        w2_sb = sb("w2_sb", [P, FC, NE, D])
        in_early[0] = True
        conv_hi = sb("conv_hi", [P, 2, TAPS, DI], f32r)
        conv_lo = sb("conv_lo", [P, 2, TAPS, DI], f32r)
        raw_w = sb("raw_w", [P, 2 * TAPS * DI])
        xi_hi = sb("xi_hi", [P, 2, SEQ + 4], f32r)
        xi_lo = sb("xi_lo", [P, 2, SEQ + 4], f32r)
        in_hi = sb("in_hi", [P, 4 * P], f32r)
        in_lo = sb("in_lo", [P, 4 * P], f32r)
        xin = sb("xin", [P, 2, NT4, D])
        xb = sb("xb", [P, NT4, D])
        xn = sb("xn", [P, SEQ])
        xn_hi = sb("xn_hi", [P, SEQ], f32r)
        xn_lo = sb("xn_lo", [P, SEQ], f32r)
        RT = sb("RT", [P, 2, 2 * SEQ])
        BCT = sb("BCT", [P, 2, SEQ])
        HT = sb("HT", [P, 2 * SEQ])
        u = sb("u", [P, 2, 2, SEQ])
        zs = sb("zs", [P, 2, 2, SEQ])
        level_mask = sb("level_mask", [P, 5, P])
        block_mask = sb("block_mask", [P, CB])
        xproj = sb("xproj", [P, 2, 2 * NST + 1])
        outproj = sb("outproj", [P, 2, D])
        nw = sb("nw", [P, 1])
        nb = sb("nb", [P, 1])
        cbias = sb("cbias", [P, 2])
        dtw = sb("dtw", [P, 2])
        dtb = sb("dtb", [P, 2])
        ndtw = sb("ndtw", [P, 2])
        ndtb = sb("ndtb", [P, 2])
        brb = sb("brb", [P, NE])
        wr_sb = sb("wr_sb", [P, NE])
        lower_f = sb("lower_f", [P, P])

        stats = sb("stats", [P, NT4, 6])
        mv1 = sb("mv1", [P, NT4, 2])
        ve1 = sb("ve1", [P, NT4])
        rs1 = sb("rs1", [P, NT4])
        mv2 = sb("mv2", [P, NT4, 2])
        ve2 = sb("ve2", [P, NT4])
        rs2 = sb("rs2", [P, NT4])
        xa = sb("xa", [P, 2, NT4, D])
        xs = sb("xs", [P, 2, NT4, 2 * NST + 1])

        dec1 = sb("dec1", [P, 2, SEQ])
        dec2 = sb("dec2", [P, 2, SEQ // 2])
        dec4 = sb("dec4", [P, 2, SEQ // 4])
        dec8 = sb("dec8", [P, 2, SEQ // 8])
        dec16 = sb("dec16", [P, 2, SEQ // 16])
        pre = sb("pre", [P, 2, SEQ])
        R = sb("R", [P, 2, SEQ])
        BC = sb("BC", [P, 2, NT4, P])
        G = sb("G", [P, 5, SEQ])
        y = sb("y", [P, 2, SEQ])
        tmp = sb("tmp", [P, 2, SEQ])
        Sall = sb("Sall", [P, 2, NST, NBLK])
        decS = sb("decS", [P, 2, NST, NBLK])
        Hs = sb("Hs", [P, 1 + 2 * NST * NBLK])
        Hp = sb("Hp", [P, 2, NT4, P])
        xr = sb("xr", [P, NT4, D])
        at = sb("at", [P, NT4, D])
        mv3 = sb("mv3", [P, NT4, 2])
        ve3 = sb("ve3", [P, NT4])
        rs3 = sb("rs3", [P, NT4])
        mv4 = sb("mv4", [P, NT4, 2])
        ve4 = sb("ve4", [P, NT4])
        rs4 = sb("rs4", [P, NT4])
        x1n = sb("x1n", [P, NT4, D])
        x1 = sb("x1", [P, NT4, D])
        xfT = sb("xfT", [P, SEQ])
        lg = sb("lg", [P, NT4, NE])
        xrow = sb("xrow", [P, 2, 2, NT4, ROW])
        top8 = sb("top8", [P, NT4, 8])
        topi8 = sb("topi8", [P, NT4, 8], u32)
        topi = sb("topi", [P, 2, NT4])
        gap = sb("gap", [P, NT4])
        chosen = sb("chosen", [P, 2, NT4, NE])
        chosen_b = sb("chosen_b", [P, NT4, NE], bf16)
        place = sb("place", [P, NT4, NE])
        placed = sb("placed", [P, 2, NT4, NE])
        pos = sb("pos", [P, 2, NT4])
        send_at = sb("send_at", [P, 2, 2, NT4], i32)
        early.close()
        in_early[0] = False
        w13_sb = sb("w13_sb", [P, NE, 2, DF])
        gb = sb("gb", [P, 2, NE, D])
        got = sb("got", [P, 4, ROW])
        got_id = sb("got_id", [P, 4], i32)
        xsT = sb("xsT", [P, 2, P])
        sil = sb("sil", [P, 2, DF])
        hid = sb("hid", [P, 2, DF])
        hidT = sb("hidT", [P, 2, DF])
        est = sb("est", [P, 6])
        emv = sb("emv", [P, 2, 2])
        eve = sb("eve", [P, 2])
        ers = sb("ers", [P, 2])
        erw = sb("erw", [P, 2])
        wb = sb("wb", [P, 2, D])
        yg = sb("yg", [P, 2, D])
        yo = sb("yo", [P, 4, D])
        fx1 = sb("fx1", [P, NG, NT4, D])
        fch = sb("fch", [P, 2, 2, NT4, D])
        facc = sb("facc", [P, 2, NT4, D])
        fst = sb("fst", [P, NT4, 6])
        fmv = sb("fmv", [P, 2, NT4, 2])
        fve = sb("fve", [P, 2, NT4])
        frs = sb("frs", [P, 2, NT4])

        pA = pb("pA", [P, 2, SEQ])
        pB = pb("pB", [P, 2, SEQ])
        pR = pb("pR", [P, 2, SEQ])
        pY = pb("pY", [P, 2, SEQ])

        w_loaded = sem("w_loaded")
        in_w_loaded = sem("in_w_loaded")
        conv_w_loaded = sem("conv_w_loaded")
        const_ready = sem("const_ready")
        dve_consts = sem("dve_consts")
        w_hi = sem("w_hi")
        w_split = sem("w_split")
        x_loaded = [sem("x_loaded0"), sem("x_loaded1")]
        xr_loaded = sem("xr_loaded")
        x1_stored = sem("x1_stored")
        ds_t = sem("ds_t")
        bc_t = sem("bc_t")
        rt_t = sem("rt_t")
        g_mm = sem("g_mm")
        y_mm = sem("y_mm")
        xt_t = sem("xt_t")
        ip_mm = sem("ip_mm")
        cv_mm = sem("cv_mm")
        xs_mm = sem("xs_mm")
        op_mm = sem("op_mm")
        xf_t = sem("xf_t")
        lg_mm = sem("lg_mm")
        dec1_ready = sem("dec1_ready")
        bct_ready = sem("bct_ready")
        rt_ready = sem("rt_ready")
        y0_ready = sem("y0_ready")
        xn_ready = sem("xn_ready")
        xi_hi_ready = sem("xi_hi_ready")
        z_ready = sem("z_ready")
        u_ready = sem("u_ready")
        xs_ready = sem("xs_ready")
        s_ready = sem("s_ready")
        decs_ready = sem("decs_ready")
        hp_ready = sem("hp_ready")
        xft_ready = sem("xft_ready")
        r_odd_ready = sem("r_odd_ready")
        pre_ready = sem("pre_ready")
        rstd_a = sem("rstd_a")
        rstd_c = sem("rstd_c")
        xn_lo_ready = sem("xn_lo_ready")
        r_ready = sem("r_ready")
        dec_ready = sem("dec_ready")
        x1_ready = sem("x1_ready")
        dve_a = sem("dve_a")
        dve_b = sem("dve_b")
        dve_c = sem("dve_c")
        var_a = sem("var_a")
        var_c = sem("var_c")
        xa_ready = sem("xa_ready")
        xb_ready = sem("xb_ready")
        xi_lo_ready = sem("xi_lo_ready")
        bc_ready = sem("bc_ready")
        g_ready = sem("g_ready")
        y_read = sem("y_read")
        hs_ready = sem("hs_ready")
        yz_ready = sem("yz_ready")
        at_ready = sem("at_ready")
        x1n_ready = sem("x1n_ready")
        xf_ready = sem("xf_ready")
        lg_read = sem("lg_read")

        halves = lambda t, h: t.rearrange("p m (b k) -> p (m b) k", k=2 * h)
        x_v = x.rearrange("s (t p) d -> s p t d", p=P)
        x1_v = x1_d.rearrange("(s t p) d -> s p t d", p=P, t=NT4)
        RANK, TOTAL = 2 * P, 2 * P + NT4 * NE
        tile = lambda t: slice(t * P, (t + 1) * P)
        TABLE_ROW = 2 * P

        blank_ready, blank_stored, e_loaded = sem("blank_ready"), sem("blank_stored"), sem("e_loaded")
        pool_passed, dve_passed = sem("pool_passed"), sem("dve_passed")
        w13_loaded = sem("w13_loaded")
        w2_loaded = sem("w2_loaded")
        gb_loaded = sem("gb_loaded")
        lower_ready = sem("lower_ready")
        stage1_pe, stage1_act, stage1_pool = sem("stage1_pe"), sem("stage1_act"), sem("stage1_pool")
        stage1_dve = sem("stage1_dve")
        stage1_sp = sem("stage1_sp")
        dve_d = sem("dve_d")
        gap_ready, chosen_ready, rank_mm = sem("gap_ready"), sem("chosen_ready"), sem("rank_mm")
        rank_read, pos_ready = sem("rank_read"), sem("pos_ready")
        weights_ready, xf2_ready, token_ready, send_at_ready = sem("weights_ready"), sem("xf2_ready"), sem("token_ready"), sem("send_at_ready")
        sent = [sem("sent0"), sem("sent1")]
        tables, tail_ready, tails_stored = sem("tables"), sem("tail_ready"), sem("tails_stored")
        cols_ready, cols_mm, table_ready = sem("cols_ready"), sem("cols_mm"), sem("table_ready")
        got_loaded = [sem(f"got_loaded{q}") for q in range(4)]
        xs_t = sem("xs_t")
        xst_ready = sem("xst_ready")
        h1_mm, h3_mm, h_t, yo_mm = sem("h1_mm"), sem("h3_mm"), sem("h_t"), sem("yo_mm")
        sil_ready, hid_ready, hidt_ready = sem("sil_ready"), sem("hid_ready"), sem("hidt_ready")
        est_c = sem("est_c")
        evar_ready, erw_ready, epow = sem("evar_ready"), sem("erw_ready"), sem("epow")
        wb_ready, yg_ready, yo_ready = sem("wb_ready"), sem("yg_ready"), sem("yo_ready")
        id_ready = sem("id_ready")
        stored = [sem(f"stored{q}") for q in range(4)]
        fx1_loaded = sem("fx1_loaded")
        f_loaded = [sem("f_loaded0"), sem("f_loaded1")]
        f_acc, f_chain, f_var, f_rstd, f_n, f_o = sem("f_acc"), sem("f_chain"), sem("f_var"), sem("f_rstd"), sem("f_n"), sem("f_o")
        f_stored = sem("f_stored")

        block = ctx.enter_context(nc.Block())

        @block.sync
        def _(eng):
            for dst, src in ((ident[:, :], ident_d), (level_mask[:, :, :], masks), (block_mask[:, :], blockmask),
                             (xproj[:, :, :], x_wT.rearrange("(m p) f -> p m f", p=P)),
                             (outproj[:, :, :], out_wT.rearrange("(m p) f -> p m f", p=P)),
                             (nw[:, :], norm_w.rearrange("(p o) -> p o", o=1)), (nb[:, :], norm_b.rearrange("(p o) -> p o", o=1)),
                             (cbias[:, 0:1], conv_b[0:P].rearrange("(p o) -> p o", o=1)), (cbias[:, 1:2], conv_b[P:DI].rearrange("(p o) -> p o", o=1)),
                             (dtw[:, 0:1], dt_w[0:P, :]), (dtw[:, 1:2], dt_w[P:DI, :]),
                             (dtb[:, 0:1], dt_b[0:P].rearrange("(p o) -> p o", o=1)), (dtb[:, 1:2], dt_b[P:DI].rearrange("(p o) -> p o", o=1)),
                             (brb[:, :], br.rearrange("(o e) -> o e", o=1).broadcast_to([P, NE])), (wr_sb[:, :], wr)):
                eng.dma_start(dst, src).then_inc(w_loaded, 16)
            eng.dma_start(raw_w[:, 0:4 * P], in_wT).then_inc(in_w_loaded, 16)

            def load_x(a):
                wait_for(eng, xa_ready, 1, a, 1, ago=2)
                eng.dma_start(xin[:, a.parity, :, :], x_v[bass.ds(a.s, 1), :, :, :].rearrange("o p t d -> (o p) t d")).then_inc(x_loaded[a.parity], 16)

            for dst, src in ((iota_es[:, :], iota_e), (slot_no[:, :], iota_p), (tokid[:, :, :], token_id), (lower_f[:, :], lower), (region_sb[:, :], region), (running[:, :], region)):
                eng.dma_start(dst, src).then_inc(e_loaded, 16)
            load_x(Seq(0, 0, 0))
            eng.wait_ge(w_split, 1)
            eng.dma_start(raw_w[:, :], conv_wT).then_inc(conv_w_loaded, 16)
            load_x(Seq(1, 0, 1))
            eng.wait_ge(blank_ready, 2)
            eng.dma_start(slots_d[BLANK:BLANK + P, :], blank[:, :]).then_inc(blank_stored, 16)
            eng.dma_start(w2_sb[:, :, :, :], w2).then_inc(w2_loaded, 16)

            def unit(a, b, c, d):
                if a is not None and not (isinstance(a.s, int) and a.s < 2):
                    load_x(a)
                if c is not None:
                    wait_for(eng, x1_ready, 1, c, 1)
                    eng.dma_start(x1_v[bass.ds(c.s, 1), :, :, :].rearrange("o p t d -> (o p) t d"), x1[:, :, :]).then_inc(x1_stored, 16)
                if b is not None:
                    wait_for(eng, x1_ready, 1, b, 1, ago=1)
                    eng.dma_start(xr[:, :, :], x_v[bass.ds(b.s, 1), :, :, :].rearrange("o p t d -> (o p) t d")).then_inc(xr_loaded, 16)

                if b is not None and a is None:
                    for q, n in ((w_split, 2), (xa_ready, NS), (xb_ready, NS), (xt_t, NS), (xn_ready, 2 * NS), (xn_lo_ready, NS), (xi_hi_ready, 2 * NS),
                                 (xi_lo_ready, 2 * NS), (ip_mm, 4 * NS), (cv_mm, 2 * NS)):
                        eng.wait_ge(q, n)
                    load_w13(0, 3 * NE // 4)
                    for q, n in ((rt_ready, 6 * NS), (bct_ready, NS), (g_mm, NS), (y_mm, 7 * NS), (yz_ready, NS), (r_ready, 4 * NS),
                                 (r_odd_ready, NS), (rt_t, 6 * NS), (z_ready, 2 * NS), (u_ready, 2 * NS), (xs_mm, NS)):
                        eng.wait_ge(q, n)
                    load_w13(3 * NE // 4, NE)
                    for k, v in enumerate((gamma, beta)):
                        eng.dma_start(gb[:, k, :, :], v.rearrange("(o e) d -> o e d", o=1).broadcast_to([P, NE, D])).then_inc(gb_loaded, 16)

            def load_w13(e0, e1):
                eng.dma_start(w13_sb[:, e0:e1, :, :], w13[:, e0:e1, :, :]).then_inc(w13_loaded, 16)

            run_units(eng, NS, unit)
            eng.wait_ge(x1_stored, 16 * NS)
            eng.nop().then_inc(stage1_sp, 1)
            for q in (stage1_pe, stage1_act, stage1_pool, stage1_dve):
                eng.wait_ge(q, 1)
            eng.wait_ge(tails_stored, 16 * NE)
            eng.wait_ge(blank_stored, 16)
            for p in range(2):
                eng.wait_ge(sent[p], NS // 2 * 2 * NT4 * 16)
            eng.wait_ge(table_ready, 1)

            def load_slots(j, q):
                row = eng.value_load(slot_table[0:1, bass.ds(j + TABLE_ROW, 1)], min_val=0, max_val=BLANK)
                eng.dma_start(got[:, q, :], slots_d[bass.ds(row, P), :]).then_inc(got_loaded[q], 16)

            for q in range(4):
                load_slots(q, q)
            eng.dma_start(fx1[:, :, :, :], x1_d.rearrange("(g t p) d -> p g t d", p=P, t=NT4)).then_inc(fx1_loaded, 16)
            with eng.Fori(1, NSLOT // 4) as j:
                for q in range(4):
                    eng.wait_ge(erw_ready, j * 4 + (q - 3))
                    eng.wait_ge(id_ready, j * 4 + (q - 3))
                    eng.wait_ge(wb_ready, j * 4 + (q - 3))
                    load_slots(j * 4 + q, q)
            for q in range(4):
                eng.wait_ge(stored[q], NSLOT // 4 * 16)
            cv = chosen_d.rearrange("(k g t p) d -> g p k t d", p=P, t=NT4, k=2)
            ov = out.rearrange("s (t p) d -> s p t d", p=P)

            def load_last(g):
                for k in range(2):
                    eng.dma_start(fch[:, g % 2, k, :, :], cv[g, :, k, :, :]).then_inc(f_loaded[g % 2], 16)

            for g in range(2):
                load_last(g)
            for g in range(NG):
                if g + 2 < NG:
                    eng.wait_ge(f_acc, g + 1)
                    load_last(g + 2)
                if g:
                    eng.wait_ge(f_o, g)
                    eng.dma_start(ov[g - 1, :, :, :], fx1[:, g - 1, :, :]).then_inc(f_stored, 16)
            eng.wait_ge(f_o, NG)
            eng.dma_start(ov[NG - 1, :, :, :], fx1[:, NG - 1, :, :]).then_inc(f_stored, 16)
            eng.wait_ge(f_stored, 16 * NG)

        @block.gpsimd
        def _(eng):
            for t, v in ((neg_half[:, :], -0.5), (xi_hi[:, :, 0:TAPS - 1].bitcast(fp32), 0.0), (xi_lo[:, :, 0:TAPS - 1].bitcast(fp32), 0.0), (decS[:, :, :, 0:1], 0.0),
                         (Hs[:, 0:1], 0.0)):
                eng.memset(t, v).then_inc(const_ready, 1)
            eng.memset(blank[:, :], 0.0).then_inc(blank_ready, 1)
            eng.wait_ge(blank_ready, 1)
            eng.memset(blank[:, D:D + 1], float(NOWHERE)).then_inc(blank_ready, 1)

            def rstd(seq, k, ve, rs, var, done):
                wait_for(eng, var, 2, seq, k)
                eng.tensor_tensor(rs[:, :], ve[:, :], neg_half[:, :], ALU.pow).then_inc(done, 1)

            decs = [dec1, dec2, dec4, dec8, dec16]

            def decay(b, n):
                h = HALVES[n]
                src = halves(R[:, :, :] if n else u[:, b.parity, :, :], h)
                d = decs[n][:, :, :].rearrange("p m (b k) -> p (m b) k", k=2)
                if n == 0:
                    wait_for(eng, dec1_ready, 1, b, 1)
                    wait_for(eng, rt_t, 6, b, 5, ago=1)
                else:
                    wait_for(eng, r_ready, 4, b, n)
                    wait_for(eng, r_odd_ready, 1, b, 1)
                    wait_for(eng, dec_ready, 4, b, n)
                    wait_for(eng, rt_t, 6, b, n + 1)
                eng.tensor_tensor(halves(R[:, :, :], h)[:, :, 0:h], src[:, :, 0:h],
                                  d[:, :, 1:2].broadcast_to([P, SEQ // h, h]), ALU.mult).then_inc(r_ready, 1)
                if n == 3:
                    wait_for(eng, decs_ready, 1, b, 1, ago=1)
                eng.tensor_tensor(decs[n + 1][:, :, :].rearrange("p m (b o) -> p (m b) o", o=1), d[:, :, 0:1], d[:, :, 1:2],
                                  ALU.mult).then_inc(dec_ready, 1)

            def send_rows(d, t):
                for k in range(2):
                    eng.indirect_dma_start(slots_d, bass.IndirectOffsetOnAxis(ap=send_at[:, d.parity, k, t:t + 1], axis=0), xrow[:, d.parity, k, t, :],
                                           None).then_inc(sent[d.parity], 16)

            def unit(a, b, c, d):
                if a is not None:
                    rstd(a, 1, ve1, rs1, var_a, rstd_a)
                if c is not None:
                    rstd(c, 1, ve3, rs3, var_c, rstd_c)
                if b is not None:
                    decay(b, 0)
                if a is not None:
                    rstd(a, 2, ve2, rs2, var_a, rstd_a)
                if d is not None:
                    wait_for(eng, xf_ready, 1, d, 1)
                    wait_for(eng, pos_ready, 1, d, 1)
                    eng.sem_inc(pool_passed, 1)
                    eng.tensor_copy(xrow[:, d.parity, :, :, D:D + 1].rearrange("p k t o -> p k (t o)"), tokid[:, :, bass.ds(d.s * NT4, NT4)]).then_inc(token_ready, 1)
                    eng.tensor_copy(send_at[:, d.parity, :, :], pos[:, :, :]).then_inc(send_at_ready, 1)
                if a is not None:
                    wait_for(eng, xn_ready, 2, a, 2)
                    wait_for(eng, ip_mm, 4, a, 4, ago=1)
                    eng.tensor_tensor(xn_lo[:, :], xn[:, :], xn_hi[:, :].bitcast(fp32), ALU.subtract).then_inc(xn_lo_ready, 1)
                if d is not None:
                    wait_for(eng, xf2_ready, 1, d, 1)
                    wait_for(eng, weights_ready, 2, d, 2)
                    wait_for(eng, token_ready, 1, d, 1)
                    wait_for(eng, send_at_ready, 1, d, 1)
                    eng.sem_inc(pool_passed, 1)
                    send_rows(d, 0)
                if b is not None:
                    decay(b, 1)
                if c is not None:
                    wait_for(eng, x1n_ready, 1, c, 1)
                    wait_for(eng, x1_stored, 16, c, 16, ago=1)
                    wait_for(eng, xr_loaded, 16, c, 16)
                    eng.tensor_tensor(x1[:, :, :], x1n[:, :, :], xr[:, :, :], ALU.add).then_inc(x1_ready, 1)
                if d is not None:
                    send_rows(d, 1)
                if b is not None:
                    decay(b, 2)
                if c is not None:
                    rstd(c, 2, ve4, rs4, var_c, rstd_c)
                if d is not None:
                    send_rows(d, 2)
                if b is not None:
                    decay(b, 3)
                if d is not None:
                    send_rows(d, 3)

            run_units(eng, NS, unit)
            eng.wait_ge(rstd_c, 2 * NS)
            eng.wait_ge(dec_ready, 4 * NS)
            eng.wait_ge(xn_lo_ready, NS)
            for p in range(2):
                eng.wait_ge(sent[p], NS // 2 * 2 * NT4 * 16)
            eng.nop().then_inc(stage1_pool, 1)

            eng.wait_ge(tail_ready, 1)
            for e in range(NE):
                eng.indirect_dma_start(slots_d, bass.IndirectOffsetOnAxis(ap=tail_at[:, e:e + 1], axis=0), blank[:, :], None).then_inc(tails_stored, 16)

            def weight(j, q):
                eng.wait_ge(evar_ready, j + 1)
                eng.tensor_tensor(ers[:, q % 2:q % 2 + 1], eve[:, q % 2:q % 2 + 1], neg_half[:, 0:1], ALU.pow).then_inc(epow, 1)
                eng.wait_ge(epow, j + 1)
                wait_past(eng, yo_ready, j - 1)
                eng.tensor_tensor(erw[:, q % 2:q % 2 + 1], ers[:, q % 2:q % 2 + 1], got[:, q, D + 1:D + 2], ALU.mult).then_inc(erw_ready, 1)

            def store(j, q):
                eng.wait_ge(yo_ready, j + 1)
                eng.wait_ge(id_ready, j + 1)
                eng.sem_inc(pool_passed, 1)
                eng.indirect_dma_start(chosen_d, bass.IndirectOffsetOnAxis(ap=got_id[:, q:q + 1], axis=0), yo[:, q, :], None,
                                       bounds_check=2 * NTOKENS - 1, oob_is_err=False).then_inc(stored[q], 16)

            def expert_tile(j, q):
                weight(j, q)
                if not (isinstance(j, int) and j < 1):
                    store(j - 1, (q - 1) % 4)

            for q in range(4):
                expert_tile(q, q)
            with eng.Fori(1, NSLOT // 4) as jj:
                for q in range(4):
                    expert_tile(jj * 4 + q, q)
            store(NSLOT - 1, 3)

            def last_add(g):
                eng.wait_ge(f_n, g + 1)
                eng.tensor_tensor(fx1[:, g, :, :], facc[:, g % 2, :, :], fx1[:, g, :, :], ALU.add).then_inc(f_o, 1)

            eng.wait_ge(fx1_loaded, 16)
            for g in range(NG):
                eng.wait_ge(f_var, g + 1)
                if g >= 2:
                    eng.wait_ge(f_n, g - 1)
                eng.tensor_tensor(frs[:, g % 2, :], fve[:, g % 2, :], neg_half[:, :], ALU.pow).then_inc(f_rstd, 1)
                if g:
                    last_add(g - 1)
            last_add(NG - 1)

        @block.scalar
        def _(eng):
            eng.wait_ge(w_loaded, 16 * 15)
            eng.wait_ge(dve_consts, 2)

            def a_xn(a):
                wait_for(eng, xt_t, 1, a, 1)
                wait_for(eng, xn_lo_ready, 1, a, 1, ago=1)
                eng.activation(xn[:, :], pA[:, 0, :], ACT.Identity, scale=nw[:, 0:1], bias=nb[:, 0:1]).then_inc(xn_ready, 1)
                wait_for(eng, ip_mm, 4, a, 4, ago=1)
                eng.activation(xn_hi[:, :], pA[:, 0, :], ACT.Identity, scale=nw[:, 0:1], bias=nb[:, 0:1]).then_inc(xn_ready, 1)

            def a_xi(a, f):
                wait_for(eng, ip_mm, 4, a, f + 1)
                wait_for(eng, cv_mm, 2, a, 2, ago=1)
                eng.activation(xi_hi[:, f, TAPS - 1:TAPS - 1 + SEQ], pA[:, 1 - f, :], ACT.Copy).then_inc(xi_hi_ready, 1)

            def a_z(a, f):
                wait_for(eng, ip_mm, 4, a, f + 3)
                wait_for(eng, yz_ready, 1, a, 1, ago=2)
                eng.activation(zs[:, a.parity, f, :], pA[:, 1 - f, :], ACT.Silu).then_inc(z_ready, 1)

            def a_u(a, f):
                wait_for(eng, cv_mm, 2, a, f + 1)
                wait_for(eng, rt_t, 6, a, 1, ago=2)
                wait_for(eng, r_odd_ready, 1, a, 1, ago=2)
                wait_for(eng, r_ready, 4, a, 1, ago=2)
                eng.activation(u[:, a.parity, f, :], pA[:, 1 - f, :], ACT.Silu, bias=cbias[:, f:f + 1]).then_inc(u_ready, 1)

            def a_xs(a):
                wait_for(eng, xs_mm, 1, a, 1)
                wait_for(eng, bc_ready, 1, a, 1, ago=2)
                wait_for(eng, ds_t, 1, a, 1, ago=2)
                eng.activation(xs[:, a.parity, :, :], pA[:, 1, 0:NT4 * 33].rearrange("p (t f) -> p t f", f=33), ACT.Copy).then_inc(xs_ready, 1)

            def b_rt(b, k):
                wait_for(eng, rt_t, 6, b, k + 1)
                if k < 2:
                    wait_for(eng, y_mm, 7, b, 5 + k, ago=1)
                else:
                    wait_for(eng, y_mm, 7, b, {2: 2, 3: 3, 4: 4}[k])
                eng.activation(RT[:, k % 2, :], pR[:, :, :].rearrange("p a b -> p (a b)"), ACT.Copy).then_inc(rt_ready, 1)

            def unit(a, b, c, d):
                if d is not None:
                    wait_for(eng, gap_ready, 1, d, 1)
                    for k in range(2):
                        eng.activation(xrow[:, d.parity, k, :, D + 1:D + 2].rearrange("p t o -> p (t o)"), gap[:, :], ACT.Sigmoid,
                                       scale=1.0 - 2 * k).then_inc(weights_ready, 1)
                if b is not None:
                    wait_for(eng, ds_t, 1, b, 1)
                    wait_for(eng, r_ready, 4, b, 1, ago=1)
                    wait_for(eng, dec_ready, 4, b, 1, ago=1)
                    wait_for(eng, pre_ready, 1, b, 1, ago=1)
                    for f in range(2):
                        i = eng.activation(dec1[:, f, :], pY[:, 0, :], ACT.Sigmoid, scale=ndtw[:, f:f + 1], bias=ndtb[:, f:f + 1])
                    i.then_inc(dec1_ready, 1)
                    wait_for(eng, bc_t, 1, b, 1)
                    wait_for(eng, y_mm, 7, b, 7, ago=1)
                    eng.activation(BCT[:, :, :], pB[:, :, :], ACT.Copy).then_inc(bct_ready, 1)
                    b_rt(b, 0)
                    wait_for(eng, rt_t, 6, b, 5, ago=1)
                    eng.activation(halves(R[:, :, :], 1)[:, :, 1:2], halves(u[:, b.parity, :, :], 1)[:, :, 1:2], ACT.Copy).then_inc(r_odd_ready, 1)
                    wait_for(eng, dec1_ready, 1, b, 1)
                    wait_for(eng, y_read, 5, b, 5, ago=1)
                    eng.activation(pre[:, :, :], dec1[:, :, :], ACT.Copy).then_inc(pre_ready, 1)
                if a is not None:
                    a_xn(a)
                if b is not None:
                    wait_for(eng, y_mm, 7, b, 1)
                    wait_for(eng, op_mm, 1, b, 1, ago=1)
                    eng.activation(y[:, :, :], pY[:, :, :], ACT.Copy).then_inc(y0_ready, 1)
                if a is not None:
                    a_xi(a, 0)
                    a_xi(a, 1)
                if b is not None:
                    b_rt(b, 1)
                if a is not None:
                    a_z(a, 0)
                    a_z(a, 1)
                if b is not None:
                    b_rt(b, 2)
                    b_rt(b, 3)
                if c is not None:
                    wait_for(eng, xf_t, 1, c, 1)
                    wait_for(eng, lg_mm, 1, c, 1, ago=1)
                    eng.activation(xfT[:, :], pB[:, 1, :], ACT.Copy).then_inc(xft_ready, 1)
                    wait_for(eng, xf_ready, 1, c, 1)
                    eng.activation(xrow[:, c.parity, 1, :, 0:D], xrow[:, c.parity, 0, :, 0:D], ACT.Copy).then_inc(xf2_ready, 1)
                if b is not None:
                    b_rt(b, 4)
                    wait_for(eng, dec_ready, 4, b, 4)
                    wait_for(eng, hs_ready, 1, b, 1, ago=1)
                    eng.activation(decS[:, :, :, 1:NBLK],
                                   dec16[:, :, 1:NBLK].rearrange("p m (o b) -> p m o b", o=1).broadcast_to([P, 2, NST, NBLK - 1]),
                                   ACT.Copy).then_inc(decs_ready, 1)
                    wait_for(eng, y_mm, 7, b, 5)
                    for m in range(2):
                        i = eng.activation(Sall[:, m, :, :].rearrange("p s (t c) -> p t s c", t=NT4), pY[:, m, :].rearrange("p (t s c) -> p t s c", t=NT4, s=NST), ACT.Copy)
                    i.then_inc(s_ready, 1)
                if a is not None:
                    a_u(a, 0)
                if b is not None:
                    wait_for(eng, hs_ready, 1, b, 1)
                    wait_for(eng, rt_t, 6, b, 6, ago=1)
                    for m in range(2):
                        i = eng.activation(Hp[:, m, :, :].rearrange("p t (s c) -> p t s c", s=NST),
                                           Hs[:, m * NST * NBLK:(m + 1) * NST * NBLK].rearrange("p (s t c) -> p t s c", s=NST, t=NT4), ACT.Copy)
                    i.then_inc(hp_ready, 1)
                    wait_for(eng, rt_t, 6, b, 6)
                    wait_for(eng, y_mm, 7, b, 7, ago=1)
                    eng.activation(HT[:, :], pR[:, :, :].rearrange("p a b -> p (a b)"), ACT.Copy).then_inc(rt_ready, 1)
                if a is not None:
                    a_u(a, 1)
                    a_xs(a)

            run_units(eng, NS, unit)
            eng.wait_ge(xs_ready, NS)
            eng.wait_ge(rt_ready, 6 * NS)
            eng.wait_ge(xft_ready, NS)
            eng.nop().then_inc(stage1_act, 1)

            for q in (stage1_pe, stage1_dve, stage1_pool, stage1_sp):
                eng.wait_ge(q, 1)
            eng.wait_ge(gb_loaded, 32)
            eng.wait_ge(table_ready, 1)

            def xst(j, p):
                eng.wait_ge(xs_t, j + 1)
                wait_past(eng, h3_mm, j - 1)
                eng.activation(xsT[:, p, :], pB[:, 0, 0:P], ACT.Copy).then_inc(xst_ready, 1)

            def weighed_beta(j, q):
                e = eng.value_load(slot_table[0:1, bass.ds(j, 1)], min_val=0, max_val=NE - 1)
                wait_past(eng, yo_ready, j - 1)
                eng.wait_ge(got_loaded[q], (j - q) * 4 + 16)
                eng.activation(wb[:, q % 2, :], gb[:, 1, bass.ds(e, 1), :].rearrange("p o d -> p (o d)"), ACT.Copy, scale=got[:, q, D + 1:D + 2]).then_inc(wb_ready, 1)

            def silu(j, p):
                eng.wait_ge(h1_mm, j + 1)
                wait_past(eng, hid_ready, j - 1)
                eng.activation(sil[:, p, :], pA[:, p, :], ACT.Silu).then_inc(sil_ready, 1)

            def hidt(j, p):
                eng.wait_ge(h_t, j + 1)
                eng.activation(hidT[:, p, :], pY[:, 0, :], ACT.Copy).then_inc(hidt_ready, 1)

            def tile_j(j, q, first=False, last=False):
                p = q % 2
                silu(j, p)
                if not first:
                    hidt(j - 1, 1 - p)
                if not last:
                    xst(j + 1, 1 - p)
                weighed_beta(j, q)

            xst(0, 0)
            for q in range(4):
                tile_j(q, q, first=q == 0)
            with eng.Fori(1, NSLOT // 4 - 1) as jj:
                for q in range(4):
                    tile_j(jj * 4 + q, q)
            for q in range(4):
                tile_j(NSLOT - 4 + q, q, last=q == 3)
            hidt(NSLOT - 1, 1)


        @block.vector
        def _(eng):
            eng.wait_ge(w_loaded, 16 * 15)
            eng.tensor_scalar(ndtw[:, :], dtw[:, :], -1.0, None, ALU.mult).then_inc(dve_consts, 1)
            eng.tensor_scalar(ndtb[:, :], dtb[:, :], -1.0, None, ALU.mult).then_inc(dve_consts, 1)
            eng.wait_ge(e_loaded, 16 * 6)
            eng.tensor_copy(lower_b[:, :], lower_f[:, :]).then_inc(lower_ready, 1)
            eng.memset(ones_b[:, :], 1.0).then_inc(lower_ready, 1)
            eng.wait_ge(in_w_loaded, 16)
            eng.tensor_copy(in_hi[:, :], raw_w[:, 0:4 * P]).then_inc(w_hi, 1)
            eng.wait_ge(w_hi, 1)
            eng.tensor_tensor(in_lo[:, :], raw_w[:, 0:4 * P], in_hi[:, :].bitcast(fp32), ALU.subtract).then_inc(w_split, 1)
            eng.wait_ge(conv_w_loaded, 16)
            flat = lambda t: t[:, :, :, :].rearrange("p m k f -> p (m k f)")
            eng.tensor_copy(flat(conv_hi), raw_w[:, :]).then_inc(w_hi, 1)
            eng.wait_ge(w_hi, 2)
            eng.tensor_tensor(flat(conv_lo), raw_w[:, :], flat(conv_hi).bitcast(fp32), ALU.subtract).then_inc(w_split, 1)

            def norm_stats(chain, seq, src, mv, ve, done):
                for t in range(NT4):
                    chain.link(eng.bn_stats(stats[:, t, :], src[:, t, :]))
                chain.wait()
                eng.sem_inc(dve_passed, 1)
                for t in range(NT4):
                    chain.link(eng.bn_aggr(mv[:, t, :], stats[:, t, :]))
                chain.wait()
                eng.tensor_scalar(ve[:, :], mv[:, :, 1:2].rearrange("p t o -> p (t o)"), EPS, None, ALU.add).then_inc(done, 1)

            def norm_apply(seq, k, dst, src, mv, rs, rstd, done):
                wait_for(eng, rstd, 2, seq, k)
                for t in range(NT4):
                    i = eng.tensor_scalar(dst[:, t, :], src[:, t, :], mv[:, t, 0:1], rs[:, t:t + 1], ALU.subtract, ALU.mult)
                i.then_inc(done, 1)

            def level(chain, b, n):
                h = HALVES[n]
                half = tmp[:, 0, :].rearrange("p (b k) -> p b k", k=h)
                wait_for(eng, y_mm, 7, b, (2, 3, 4, 6)[n])
                eng.tensor_tensor(half, halves(pY[:, :, :], h)[:, :, h:2 * h], halves(pre[:, :, :], h)[:, :, h:2 * h], ALU.mult).then_inc(y_read, 1)
                wait_for(eng, y_read, 5, b, n + 1)
                yr = halves(y[:, :, :], h)[:, :, h:2 * h]
                chain.link(eng.tensor_tensor(yr, yr, half, ALU.add))
                pr = halves(pre[:, :, :], h)
                chain.step(eng.tensor_tensor(pr[:, :, h:2 * h], pr[:, :, h:2 * h], pr[:, :, h - 1:h].broadcast_to([P, SEQ // h, h]), ALU.mult))

            def unit(a, b, c, d):
                ca, cb, cc = (Chain(eng, q, n, seq) for q, n, seq in ((dve_a, 16, a), (dve_b, 10, b), (dve_c, 26, c)))
                cd = Chain(eng, dve_d, 2, d)
                if b is not None:
                    wait_for(eng, xs_ready, 1, b, 1)
                    wait_for(eng, bc_t, 1, b, 1, ago=1)
                    wait_for(eng, y_mm, 7, b, 5, ago=1)
                    for k in range(2):
                        i = eng.tensor_tensor(BC[:, k, :, :].rearrange("p t (s c) -> p t s c", s=NST),
                                              xs[:, b.parity, :, 1 + k * NST:1 + (k + 1) * NST].rearrange("p t (s o) -> p t s o", o=1).broadcast_to([P, NT4, NST, CB]),
                                              block_mask[:, :].rearrange("p (a o c) -> p a o c", a=1, o=1).broadcast_to([P, NT4, NST, CB]), ALU.mult)
                    i.then_inc(bc_ready, 1)
                if a is not None:
                    eng.wait_ge(x_loaded[a.parity], a.half * 16 + 16)
                    norm_stats(ca, a, xin[:, a.parity, :, :], mv1, ve1, var_a)
                if c is not None:
                    wait_for(eng, at_ready, 1, c, 1)
                    norm_stats(cc, c, at, mv3, ve3, var_c)
                if d is not None:
                    wait_for(eng, rank_mm, 1, d, 1)
                    cd.step(eng.tensor_tensor(place[:, :, :], pA[:, 1, RANK:TOTAL].rearrange("p (t e) -> p t e", e=NE),
                                              running[:, :].rearrange("p (o e) -> p o e", o=1).broadcast_to([P, NT4, NE]), ALU.add))
                    wait_for(eng, rank_read, 1, d, 1, ago=1)
                    eng.tensor_tensor(running[:, :], running[:, :], pA[:, 1, TOTAL:TOTAL + NE], ALU.add).then_inc(rank_read, 1)
                    cd.step(eng.tensor_tensor(placed[:, :, :, :], chosen[:, :, :, :],
                                              place[:, :, :].rearrange("p (o t) e -> p o t e", o=1).broadcast_to([P, 2, NT4, NE]), ALU.mult))
                    cd.end()
                    wait_for(eng, send_at_ready, 1, d, 1, ago=1)
                    eng.tensor_reduce(pos[:, :, :], placed[:, :, :, :], AX.X, ALU.add).then_inc(pos_ready, 1)
                if a is not None:
                    wait_for(eng, at_ready, 1, a, 1, ago=2)
                    norm_apply(a, 1, xa[:, a.parity, :, :], xin[:, a.parity, :, :], mv1, rs1, rstd_a, xa_ready)
                    wait_for(eng, xa_ready, 1, a, 1)
                    wait_for(eng, xb_ready, 1, a, 1, ago=1)
                    norm_stats(ca, a, xa[:, a.parity, :, :], mv2, ve2, var_a)
                    ca.end()
                if b is not None:
                    wait_for(eng, g_mm, 1, b, 1)
                    wait_for(eng, y_mm, 7, b, 6, ago=1)
                    for n in range(5):
                        i = eng.tensor_tensor(G[:, n, :].rearrange("p (t r) -> p t r", t=NT4), pB[:, 0, :].rearrange("p (t r) -> p t r", t=NT4),
                                              level_mask[:, n:n + 1, :].broadcast_to([P, NT4, P]), ALU.mult)
                    i.then_inc(g_ready, 1)
                if c is not None:
                    wait_for(eng, x1_ready, 1, c, 1, ago=1)
                    norm_apply(c, 1, x1n, at, mv3, rs3, rstd_c, x1n_ready)
                if a is not None:
                    wait_for(eng, xt_t, 1, a, 1, ago=1)
                    norm_apply(a, 2, xb, xa[:, a.parity, :, :], mv2, rs2, rstd_a, xb_ready)
                if b is not None:
                    wait_for(eng, y0_ready, 1, b, 1)
                    wait_for(eng, pre_ready, 1, b, 1)
                    level(cb, b, 0)
                if a is not None:
                    for f in range(2):
                        wait_for(eng, xi_hi_ready, 2, a, f + 1)
                        wait_for(eng, cv_mm, 2, a, 2, ago=1)
                        w = slice(TAPS - 1, TAPS - 1 + SEQ)
                        eng.tensor_tensor(xi_lo[:, f, w], pA[:, 1 - f, :], xi_hi[:, f, w].bitcast(fp32), ALU.subtract).then_inc(xi_lo_ready, 1)
                if c is not None:
                    wait_for(eng, x1_ready, 1, c, 1)
                    wait_for(eng, xf_ready, 1, c, 1, ago=1)
                    norm_stats(cc, c, x1, mv4, ve4, var_c)
                if b is not None:
                    level(cb, b, 1)
                if c is not None:
                    wait_for(eng, xf_t, 1, c, 1, ago=1)
                    if not (isinstance(c.s, int) and c.s < 2):
                        eng.wait_ge(sent[c.parity], c.half * (2 * NT4 * 16))
                    norm_apply(c, 2, xrow[:, c.parity, 0, :, 0:D], x1, mv4, rs4, rstd_c, xf_ready)
                if b is not None:
                    level(cb, b, 2)
                    wait_for(eng, s_ready, 1, b, 1)
                    wait_for(eng, decs_ready, 1, b, 1)
                    wait_for(eng, hp_ready, 1, b, 1, ago=1)
                    cb.step(eng.tensor_tensor_scan(Hs[:, 1:1 + 2 * NST * NBLK], decS[:, :, :, :].rearrange("p m s b -> p (m s b)"),
                                                   Sall[:, :, :, :].rearrange("p m s b -> p (m s b)"), 0.0, ALU.mult, ALU.add))
                    eng.memset(Hs[:, 0:2 * NST * NBLK].rearrange("p (r b) -> p r b", b=NBLK)[:, :, 0:1], 0.0).then_inc(hs_ready, 1)
                if c is not None:
                    wait_for(eng, lg_mm, 1, c, 1)
                    eng.tensor_tensor(lg[:, :, :], pB[:, 1, 0:NT4 * NE].rearrange("p (t e) -> p t e", e=NE),
                                      brb[:, :].rearrange("p (o e) -> p o e", o=1).broadcast_to([P, NT4, NE]), ALU.add).then_inc(lg_read, 1)
                    wait_for(eng, lg_read, 1, c, 1)
                    eng.sem_inc(dve_passed, 1)
                    for t in range(NT4):
                        cc.link(eng.max(top8[:, t, :], lg[:, t, :]))
                    cc.wait()
                    wait_for(eng, weights_ready, 2, c, 2, ago=1)
                    eng.tensor_tensor(gap[:, :], top8[:, :, 0:1].rearrange("p t o -> p (t o)"), top8[:, :, 1:2].rearrange("p t o -> p (t o)"),
                                      ALU.subtract).then_inc(gap_ready, 1)
                    for t in range(NT4):
                        cc.link(eng.max_index(topi8[:, t, :], top8[:, t, :], lg[:, t, :]))
                    cc.wait()
                    cc.step(eng.tensor_copy(topi[:, :, :], topi8[:, :, 0:2].rearrange("p t k -> p k t")))
                    cc.step(eng.tensor_tensor(chosen[:, :, :, :], iota_es[:, :].rearrange("p (a o e) -> p a o e", a=1, o=1).broadcast_to([P, 2, NT4, NE]),
                                              topi[:, :, :].rearrange("p k (t o) -> p k t o", o=1).broadcast_to([P, 2, NT4, NE]), ALU.is_equal))
                    wait_for(eng, rank_mm, 1, c, 1, ago=1)
                    eng.tensor_tensor(chosen_b[:, :, :], chosen[:, 0, :, :], chosen[:, 1, :, :], ALU.add).then_inc(chosen_ready, 1)
                    cc.end()
                if b is not None:
                    level(cb, b, 3)
                    wait_for(eng, y_mm, 7, b, 7)
                    eng.tensor_tensor(tmp[:, :, :], pY[:, :, :], pre[:, :, :], ALU.mult).then_inc(y_read, 1)
                    wait_for(eng, y_read, 5, b, 5)
                    cb.step(eng.tensor_tensor(y[:, :, :], y[:, :, :], tmp[:, :, :], ALU.add))
                    cb.end()
                    wait_for(eng, z_ready, 2, b, 2)
                    eng.tensor_tensor(y[:, :, :], y[:, :, :], zs[:, b.parity, :, :], ALU.mult).then_inc(yz_ready, 1)
                    wait_for(eng, op_mm, 1, b, 1)
                    wait_for(eng, x1n_ready, 1, b, 1, ago=1)
                    eng.tensor_tensor(at[:, :, :], pB[:, 0, :].rearrange("p (t d) -> p t d", t=NT4), xa[:, b.parity, :, :], ALU.add).then_inc(at_ready, 1)

            run_units(eng, NS, unit)
            eng.wait_ge(at_ready, NS)
            eng.wait_ge(xf_ready, NS)
            eng.wait_ge(yz_ready, NS)
            eng.wait_ge(pos_ready, NS)
            eng.nop().then_inc(stage1_dve, 1)

            eng.wait_ge(rank_read, NS)
            r = Chain(eng, tables, 0, Seq(0, 0, 0))
            r.link(eng.tensor_tensor(count_i[:, :], running[:, :], region_sb[:, :], ALU.subtract))
            eng.tensor_scalar(tail_at[:, :], running[:, :], slot_no[:, 0:1], None, ALU.add).then_inc(tail_ready, 1)
            r.link(eng.memset(ones_e[:, :], 1.0))
            r.step(eng.memset(shift_step[:, NE - 1:NE], float(NOWHERE)))
            r.step(eng.tensor_scalar(count_i[:, :], count_i[:, :], P - 1, None, ALU.add))
            r.step(eng.tensor_scalar(ntiles_i[:, :], count_i[:, :], P.bit_length() - 1, None, ALU.arith_shift_right))
            r.step(eng.tensor_copy(ntiles[:, :], ntiles_i[:, :]))
            r.step(eng.tensor_tensor_scan(tiles_to[:, :], ones_e[:, :], ntiles[:, :], 0.0, ALU.mult, ALU.add))
            r.step(eng.tensor_tensor(before[:, :], tiles_to[:, :], ntiles[:, :], ALU.subtract))
            r.step(eng.scalar_tensor_tensor(out=shift[:, :], in0=before[:, :], scalar=-float(P), in1=region_sb[:, :], op0=ALU.mult, op1=ALU.add))
            r.step(eng.tensor_tensor(shift_step[:, 0:NE - 1], shift[:, 1:NE], shift[:, 0:NE - 1], ALU.subtract))
            r.step(eng.tensor_tensor(past[:, :, :], slot_no[:, :].rearrange("p (c o) -> p c o", o=1).broadcast_to([P, 2, NE]),
                                     tiles_to[:, :].rearrange("p (o e) -> p o e", o=1).broadcast_to([P, 2, NE]), ALU.is_ge))
            r.step(eng.tensor_tensor(past_step[:, :, :], past[:, :, :], shift_step[:, :].rearrange("p (o e) -> p o e", o=1).broadcast_to([P, 2, NE]), ALU.mult))
            r.link(eng.tensor_reduce(slot_cols[:, 0:2], past[:, :, :], AX.X, ALU.add))
            r.step(eng.tensor_reduce(slot_cols[:, 2:4], past_step[:, :, :], AX.X, ALU.add))
            r.step(eng.scalar_tensor_tensor(out=slot_cols[:, 2:4], in0=slot_no[:, :], scalar=float(P), in1=slot_cols[:, 2:4], op0=ALU.mult, op1=ALU.add))
            eng.tensor_scalar(slot_cols[:, 0:2], slot_cols[:, 0:2], float(NE - 1), None, ALU.min).then_inc(cols_ready, 1)
            eng.tensor_scalar(slot_cols[:, 2:4], slot_cols[:, 2:4], float(BLANK), None, ALU.min).then_inc(cols_ready, 1)
            eng.wait_ge(cols_mm, 1)
            eng.tensor_copy(slot_table[:, :], pA[0:1, 0, :]).then_inc(table_ready, 1)
            for q in (stage1_pe, stage1_act, stage1_pool, stage1_sp):
                eng.wait_ge(q, 1)
            eng.wait_ge(gb_loaded, 32)

            def mult(j, p):
                eng.wait_ge(sil_ready, j + 1)
                eng.wait_ge(h3_mm, j + 1)
                wait_past(eng, h_t, j - 1)
                eng.tensor_tensor(hid[:, p, :], pR[:, p, :], sil[:, p, :], ALU.mult).then_inc(hid_ready, 1)

            def normalise(j, q):
                p = q % 2
                e = eng.value_load(slot_table[0:1, bass.ds(j, 1)], min_val=0, max_val=NE - 1)
                eng.wait_ge(yo_mm, j + 1)
                c = Chain(eng, est_c, 2, Seq(j, 0, 0))
                c.step(eng.bn_stats(est[:, :], (pB, pY)[p][:, 1, 0:D]))
                eng.sem_inc(dve_passed, 1)
                c.step(eng.bn_aggr(emv[:, p, :], est[:, :]))
                wait_past(eng, epow, j - 1)
                eng.tensor_scalar(eve[:, p:p + 1], emv[:, p, 1:2], EPS, None, ALU.add).then_inc(evar_ready, 1)
                eng.scalar_tensor_tensor(out=yg[:, p, :], in0=(pB, pY)[p][:, 1, 0:D], scalar=emv[:, p, 0:1], in1=gb[:, 0, bass.ds(e, 1), :].rearrange("p o d -> p (o d)"),
                                         op0=ALU.subtract, op1=ALU.mult).then_inc(yg_ready, 1)
                wait_past(eng, stored[q], (j - q) * 4)
                eng.tensor_copy(got_id[:, q:q + 1], got[:, q, D:D + 1]).then_inc(id_ready, 1)

            def weigh(j, q):
                p = q % 2
                eng.wait_ge(erw_ready, j + 1)
                eng.wait_ge(wb_ready, j + 1)
                eng.wait_ge(yg_ready, j + 1)
                eng.scalar_tensor_tensor(out=yo[:, q, :], in0=yg[:, p, :], scalar=erw[:, p:p + 1], in1=wb[:, p, :],
                                         op0=ALU.mult, op1=ALU.add).then_inc(yo_ready, 1)

            def tile_j(j, q, n=2):
                mult(j, q % 2)
                if n > 0:
                    normalise(j - 1, (q - 1) % 4)
                if n > 1:
                    weigh(j - 2, (q - 2) % 4)

            for q in range(4):
                tile_j(q, q, n=q)
            with eng.Fori(1, NSLOT // 4) as jj:
                for q in range(4):
                    tile_j(jj * 4 + q, q)
            normalise(NSLOT - 1, 3)
            weigh(NSLOT - 2, 2)
            weigh(NSLOT - 1, 3)

            def last_apply(g):
                p = g % 2
                eng.wait_ge(f_rstd, g + 1)
                for t in range(NT4):
                    i = eng.tensor_scalar(facc[:, p, t, :], facc[:, p, t, :], fmv[:, p, t, 0:1], frs[:, p, t:t + 1], ALU.subtract, ALU.mult)
                i.then_inc(f_n, 1)

            for g in range(NG):
                p = g % 2
                c = Chain(eng, f_chain, 8, Seq(g, 0, 0))
                eng.wait_ge(f_loaded[p], 32 * (g // 2 + 1))
                if g >= 2:
                    eng.wait_ge(f_o, g - 1)
                eng.tensor_tensor(facc[:, p, :, :], fch[:, p, 0, :, :], fch[:, p, 1, :, :], ALU.add).then_inc(f_acc, 1)
                eng.wait_ge(f_acc, g + 1)
                for t in range(NT4):
                    c.link(eng.bn_stats(fst[:, t, :], facc[:, p, t, :]))
                c.wait()
                for t in range(NT4):
                    c.link(eng.bn_aggr(fmv[:, p, t, :], fst[:, t, :]))
                c.wait()
                eng.tensor_scalar(fve[:, p, :], fmv[:, p, :, 1:2].rearrange("p t o -> p (t o)"), EPS, None, ALU.add).then_inc(f_var, 1)
                if g:
                    last_apply(g - 1)
            last_apply(NG - 1)

        @block.tensor
        def _(eng):
            eng.wait_ge(w_loaded, 16 * 15)
            eng.wait_ge(w_split, 2)
            eng.wait_ge(const_ready, 5)

            def split_mm(out, hi, lo, x_hi, x_lo, start, stop):
                eng.matmul(out, hi, x_hi, start=start, stop=False)
                eng.matmul(out, hi, x_lo, start=False, stop=False)
                return eng.matmul(out, lo, x_hi, start=False, stop=stop)

            def b_rt(b, k, src):
                if k:
                    wait_for(eng, rt_ready, 6, b, k)
                else:
                    wait_for(eng, rt_ready, 6, b, 6, ago=1)
                for t in range(NT4):
                    for m in range(2):
                        i = eng.transpose(pR[:, t // 2, (t % 2) * DI + m * P:(t % 2) * DI + (m + 1) * P], src(m, t), ident[:, :])
                i.then_inc(rt_t, 1)

            def b_y(b, k, n, free):
                wait_for(eng, rt_ready, 6, b, k + 1)
                free()
                for m in range(2):
                    for t in range(NT4):
                        i = eng.matmul(pY[:, m, tile(t)], RT[:, k % 2, t * DI + m * P:t * DI + (m + 1) * P], G[:, n, tile(t)], start=True, stop=True)
                i.then_inc(y_mm, 1)

            def a_in(a, f, d):
                if f == 0:
                    wait_for(eng, xn_lo_ready, 1, a, 1)
                    wait_for(eng, xs_ready, 1, a, 1, ago=1)
                    if d is not None:
                        wait_for(eng, rank_read, 1, d, 1)
                elif f > 1:
                    wait_for(eng, xi_hi_ready, 2, a, f - 1)
                    wait_for(eng, xi_lo_ready, 2, a, f - 1)
                split_mm(pA[:, 1 - f % 2, :], in_hi[:, tile(f)], in_lo[:, tile(f)], xn_hi[:, :], xn_lo[:, :], True, True).then_inc(ip_mm, 1)

            def a_conv(a, f, part):
                if part == 0:
                    wait_for(eng, z_ready, 2, a, f + 1)
                for k in range(TAPS):
                    w = slice(k, k + SEQ)
                    i = split_mm(pA[:, 1 - f, :], conv_hi[:, part, k, tile(f)], conv_lo[:, part, k, tile(f)], xi_hi[:, part, w], xi_lo[:, part, w],
                                 part == 0 and k == 0, part == 1 and k == TAPS - 1)
                if part:
                    i.then_inc(cv_mm, 1)

            def unit(a, b, c, d):
                if b is not None:
                    wait_for(eng, xs_ready, 1, b, 1)
                    wait_for(eng, y_read, 5, b, 5, ago=1)
                    for t in range(NT4):
                        i = eng.transpose(pY[:, 0, tile(t)], xs[:, b.parity, t, 0:1].broadcast_to([P, P]), ident[:, :])
                    i.then_inc(ds_t, 1)
                    wait_for(eng, bc_ready, 1, b, 1)
                    wait_for(eng, at_ready, 1, b, 1, ago=1)
                    if c is not None:
                        wait_for(eng, lg_read, 1, c, 1, ago=1)
                    for k in range(2):
                        for t in range(NT4):
                            i = eng.transpose(pB[:, k, tile(t)], BC[:, k, t, :], ident[:, :])
                    i.then_inc(bc_t, 1)
                    wait_for(eng, u_ready, 2, b, 2)
                    b_rt(b, 0, lambda m, t: u[:, b.parity, m, tile(t)])
                    wait_for(eng, bct_ready, 1, b, 1)
                    for t in range(NT4):
                        i = eng.matmul(pB[:, 0, tile(t)], BCT[:, 0, tile(t)], BCT[:, 1, tile(t)], start=True, stop=True)
                    i.then_inc(g_mm, 1)
                if a is not None:
                    wait_for(eng, xb_ready, 1, a, 1)
                    wait_for(eng, u_ready, 2, a, 2, ago=1)
                    for t in range(NT4):
                        i = eng.transpose(pA[:, 0, tile(t)], xb[:, t, :], ident[:, :])
                    i.then_inc(xt_t, 1)
                if b is not None:
                    wait_for(eng, g_ready, 1, b, 1)
                    b_y(b, 0, 4, lambda: wait_for(eng, dec1_ready, 1, b, 1))
                if a is not None:
                    a_in(a, 0, d)
                    a_in(a, 1, d)
                src = lambda m, t: R[:, m, tile(t)]
                if b is not None:
                    wait_for(eng, r_ready, 4, b, 1)
                    wait_for(eng, r_odd_ready, 1, b, 1)
                    b_rt(b, 1, src)
                    b_y(b, 0, 0, lambda: wait_for(eng, y0_ready, 1, b, 1))
                if a is not None:
                    a_in(a, 2, d)
                    a_in(a, 3, d)
                if b is not None:
                    wait_for(eng, r_ready, 4, b, 2)
                    b_rt(b, 2, src)
                    b_y(b, 1, 1, lambda: wait_for(eng, y_read, 5, b, 1))
                if a is not None:
                    a_conv(a, 0, 0)
                if b is not None:
                    wait_for(eng, r_ready, 4, b, 3)
                    b_rt(b, 3, src)
                    b_y(b, 2, 2, lambda: wait_for(eng, y_read, 5, b, 2))
                if c is not None:
                    wait_for(eng, xf_ready, 1, c, 1)
                    if b is not None:
                        wait_for(eng, bct_ready, 1, b, 1)
                    else:
                        wait_for(eng, lg_read, 1, c, 1, ago=1)
                    for t in range(NT4):
                        i = eng.transpose(pB[:, 1, tile(t)], xrow[:, c.parity, 0, t, 0:D], ident[:, :])
                    i.then_inc(xf_t, 1)
                if a is not None:
                    a_conv(a, 0, 1)
                if b is not None:
                    wait_for(eng, r_ready, 4, b, 4)
                    b_rt(b, 4, src)
                    wait_for(eng, rt_ready, 6, b, 5)
                    wait_for(eng, y_read, 5, b, 3)
                    for m in range(2):
                        for t in range(NT4):
                            i = eng.matmul(pY[:, m, tile(t)], RT[:, 0, t * DI + m * P:t * DI + (m + 1) * P], BC[:, 0, t, :], start=True, stop=True)
                    i.then_inc(y_mm, 1)
                if a is not None:
                    a_conv(a, 1, 0)
                if c is not None:
                    wait_for(eng, xft_ready, 1, c, 1)
                    for t in range(NT4):
                        i = eng.matmul(pB[:, 1, t * NE:(t + 1) * NE], xfT[:, tile(t)], wr_sb[:, :], start=True, stop=True)
                    i.then_inc(lg_mm, 1)
                if b is not None:
                    b_y(b, 3, 3, lambda: wait_for(eng, s_ready, 1, b, 1))
                if a is not None:
                    a_conv(a, 1, 1)
                if b is not None:
                    wait_for(eng, hp_ready, 1, b, 1)
                    b_rt(b, 5, lambda m, t: Hp[:, m, t, :])
                    wait_for(eng, rt_ready, 6, b, 6)
                    wait_for(eng, y_read, 5, b, 4)
                    for m in range(2):
                        for t in range(NT4):
                            i = eng.matmul(pY[:, m, tile(t)], HT[:, t * DI + m * P:t * DI + (m + 1) * P], BCT[:, 1, tile(t)], start=True, stop=True)
                    i.then_inc(y_mm, 1)
                if a is not None:
                    wait_for(eng, u_ready, 2, a, 2)
                    for t in range(NT4):
                        for m in range(2):
                            i = eng.matmul(pA[:, 1, t * 33:(t + 1) * 33], u[:, a.parity, m, tile(t)], xproj[:, m, :], start=m == 0, stop=m == 1)
                    i.then_inc(xs_mm, 1)
                if b is not None:
                    wait_for(eng, yz_ready, 1, b, 1)
                    for t in range(NT4):
                        for m in range(2):
                            i = eng.matmul(pB[:, 0, tile(t)], y[:, m, tile(t)], outproj[:, m, :], start=m == 0, stop=m == 1)
                    i.then_inc(op_mm, 1)
                if c is not None:
                    wait_for(eng, chosen_ready, 1, c, 1)
                    wait_for(eng, rank_read, 1, c, 1, ago=1)
                    wait_for(eng, xs_ready, 1, c if a is None else a, 1)
                    for t in range(NT4 + 1):
                        r = pA[:, 1, RANK + t * NE:RANK + (t + 1) * NE]
                        for n in range(min(t + 1, NT4)):
                            i = eng.matmul(r, (lower_b if n == t else ones_b)[:, :], chosen_b[:, n, :], start=n == 0, stop=n == min(t, NT4 - 1))
                    i.then_inc(rank_mm, 1)

            run_units(eng, NS, unit)
            eng.wait_ge(op_mm, NS)
            eng.wait_ge(lg_mm, NS)
            eng.nop().then_inc(stage1_pe, 1)

            eng.wait_ge(cols_ready, 2)
            for n in range(4):
                i = eng.matmul(pA[0:1, 0, tile(n)], slot_cols[:, n:n + 1], ident[:, :], start=True, stop=True)
            i.then_inc(cols_mm, 1)

            eng.wait_ge(w13_loaded, 32)
            eng.wait_ge(w2_loaded, 16)
            for q in (stage1_act, stage1_dve):
                eng.wait_ge(q, 1)
            eng.wait_ge(table_ready, 1)

            def x_t(j, q):
                eng.wait_ge(got_loaded[q], (j - q) * 4 + 16)
                wait_past(eng, xst_ready, j)
                eng.transpose(pB[:, 0, 0:P], got[:, q, 0:D], ident[:, :]).then_inc(xs_t, 1)

            def up(j, p, e, k, out, free, done):
                if k == 0:
                    eng.wait_ge(xst_ready, j + 1)
                wait_past(eng, free, j - 1)
                eng.matmul(out[:, p, :], xsT[:, p, :], w13_sb[:, bass.ds(e, 1), k, :].rearrange("p o f -> p (o f)"), start=True, stop=True).then_inc(done, 1)

            def hid_t(j, p):
                eng.wait_ge(hid_ready, j + 1)
                wait_past(eng, hidt_ready, j)
                for c in range(FC):
                    i = eng.transpose(pY[:, 0, tile(c)], hid[:, p, tile(c)], ident[:, :])
                i.then_inc(h_t, 1)

            def down(j, p, e):
                eng.wait_ge(hidt_ready, j + 1)
                wait_past(eng, yg_ready, j - 1)
                for c in range(FC):
                    i = eng.matmul((pB, pY)[p][:, 1, 0:D], hidT[:, p, tile(c)], w2_sb[:, c, bass.ds(e, 1), :].rearrange("p o d -> p (o d)"), start=c == 0, stop=c == FC - 1)
                i.then_inc(yo_mm, 1)

            expert_of = lambda j: eng.value_load(slot_table[0:1, bass.ds(j, 1)], min_val=0, max_val=NE - 1)

            def tile_j(j, q, before, last=False):
                p = q % 2
                e = expert_of(j)
                up(j, p, e, 0, pA, sil_ready, h1_mm)
                if before is not None:
                    hid_t(j - 1, 1 - p)
                up(j, p, e, 1, pR, hid_ready, h3_mm)
                if not last:
                    x_t(j + 1, (q + 1) % 4)
                if before is not None:
                    down(j - 1, 1 - p, before)
                return e

            x_t(0, 0)
            e = None
            for q in range(4):
                e = tile_j(q, q, e)
            with eng.Fori(1, NSLOT // 4 - 1) as jj:
                e = expert_of(jj * 4 - 1)
                for q in range(4):
                    e = tile_j(jj * 4 + q, q, e)
            e = expert_of(NSLOT - 5)
            for q in range(4):
                e = tile_j(NSLOT - 4 + q, q, e, last=q == 3)
            hid_t(NSLOT - 1, 1)
            down(NSLOT - 1, 1, e)


_INS = ['x', 'norm_w', 'norm_b', 'in_wT', 'conv_wT', 'conv_b', 'x_wT', 'dt_w', 'dt_b', 'out_wT', 'masks', 'blockmask', 'ident', 'br', 'wr', 'w13', 'w2', 'gamma', 'beta', 'lower', 'iota_e', 'iota_p', 'region', 'token_id']


def kernel(**inputs):
    import numpy as _np
    import concourse.bacc as _bacc
    from concourse import mybir as _mybir
    from concourse.bass_utils import run_bass_kernel_spmd as _run
    nc = _bacc.Bacc("TRN2", target_bir_lowering=False, num_devices=1)
    g = {k.replace('L0_attn_', '').replace('L0_ffn_', 'f_'): _np.asarray(v) for k, v in inputs.items()}
    r = _np.arange(128)
    masks = _np.stack([((r[:, None] // (2 * h) == r[None, :] // (2 * h)) & (r[:, None] % (2 * h) < h) & (r[None, :] % (2 * h) >= h)) for h in (1, 2, 4, 8)]
                      + [r[:, None] == r[None, :]], 1).astype(_np.float32)
    d = {'x': g['x'], 'norm_w': g['norm_w'], 'norm_b': g['norm_b'], 'in_wT': g['in_proj_w'].T,
         'conv_wT': g['conv_w'].reshape(256, 2, 128, 4).transpose(2, 1, 3, 0).reshape(128, -1), 'conv_b': g['conv_b'],
         'x_wT': g['x_proj_w'].T, 'dt_w': g['dt_w'], 'dt_b': g['dt_b'], 'out_wT': g['out_proj_w'].T,
         'masks': masks, 'blockmask': (r[:, None] // 16 == _np.arange(8)[None]).astype(_np.float32), 'ident': _np.eye(128, dtype=_np.float32),
         'br': g['f_br'], 'wr': g['f_Wr']}
    NS = g['x'].shape[0]
    d['w13'] = _np.stack([g['f_W1'], g['f_W3']], 1).transpose(2, 0, 1, 3)
    d['w2'] = g['f_W2'].reshape(16, 4, 128, 128).transpose(2, 1, 0, 3)
    d['gamma'], d['beta'] = g['f_gamma'], g['f_beta']
    d['lower'] = (r[:, None] < r[None, :]).astype(_np.float32)
    d['iota_e'] = _np.tile(_np.arange(16, dtype=_np.float32)[None], (128, 1))
    tokens = NS * 512
    d['iota_p'] = (r[:, None] + 128 * _np.arange(2)[None]).astype(_np.float32)
    d['region'] = _np.tile((_np.arange(16, dtype=_np.float32) * (tokens + 128))[None], (128, 1))
    d['token_id'] = (r[:, None, None] + 128 * _np.arange(NS * 4)[None, None] + tokens * _np.arange(2)[None, :, None]).astype(_np.float32)
    _OUTS = [((NS, 512, 128), 'float32')]
    arrays, args = {}, []
    for name in _INS:
        a = _np.ascontiguousarray(d[name])
        arrays[f"in_{name}_dram"] = a
        args.append(nc.dram_tensor(f"in_{name}_dram", a.shape, _mybir.dt.from_np(a.dtype), kind="ExternalInput").ap())
    for i, (shape, dtype) in enumerate(_OUTS):
        args.append(nc.dram_tensor(f"out_{i}_dram", shape, _mybir.dt.from_np(_np.dtype(dtype)), kind="ExternalOutput").ap())
    sandwich(nc, NS, *args)
    r = _run(nc, [arrays], core_ids=[0])
    return r.results[0]["out_0_dram"]
```
